# Optimizing a Trainium2 kernel written in Bass

```python
import numpy as np
import jax
import jax.numpy as jnp

def _softmax(x, axis=-1):
    return jax.nn.softmax(x, axis=axis)
def _gelu(x):
    return jax.nn.gelu(x, approximate=True)
def _silu(x):
    return jax.nn.silu(x)
def _sigmoid(x):
    return jax.nn.sigmoid(x)
def _layernorm(x, axis=-1, eps=1e-5):
    m = jnp.mean(x, axis=axis, keepdims=True)
    v = jnp.var(x, axis=axis, keepdims=True)
    return (x - m) / jnp.sqrt(v + eps)
def _scatter_add(tgt, idx, src, axis=0):
    return tgt.at[idx].add(src)
def _segment_sum(src, seg, n):
    return jax.ops.segment_sum(src, seg, n)

kernel_name = 'mk_adj_preln_d4_adj_128_38d3dd'

def setup_inputs(seed: int = 0):
    np.random.seed(seed)
    _w = jnp.asarray
    def _rec_inputs():
        import jax
        import jax.numpy as jnp
        _gk = jax.random.key(seed)
        x = -0.003407 + 1.001 * jax.random.normal(jax.random.fold_in(_gk, 1), (64, 256, 128), jnp.float32)
        _w = (1.0 + jnp.arange(256, dtype=jnp.float32)) ** -0.5
        _w = _w / _w.mean()
        _pij = jnp.clip(0.015625 * _w[:, None] * _w[None, :], 0.0, 1.0)
        _a = jax.random.uniform(jax.random.fold_in(_gk, 2), (256, 256)) < _pij
        _a = jnp.logical_or(_a, jnp.swapaxes(_a, -1, -2))
        _a = jnp.logical_or(_a, jnp.eye(256, dtype=bool))
        _af = _a.astype(jnp.float32)
        _af = _af * jax.random.uniform(jax.random.fold_in(_gk, 3), (256, 256), jnp.float32, 0.05, 0.27663)
        adj = _af
        return x, adj
    x, adj = _rec_inputs()
    def _L0_gnn_setup():
        import jax, jax.numpy as jnp
        import numpy as np
        ALPHA = 0.2
        F_DIM = 128
        key = jax.random.key(seed)
        k1, k2, k3, k4 = jax.random.split(key, 4)
        B, K, F = (4, 256, F_DIM)
        E2 = 2 * F
        x = jax.random.normal(k1, (B, K, F), dtype=jnp.float32)
        W = jax.random.normal(k2, (E2, 2 * F), dtype=jnp.float32) * np.sqrt(2.0 / (E2 + 2 * F))
        b_lin = jnp.zeros((E2,), dtype=jnp.float32)
        limit = 1.414 * np.sqrt(6.0 / (E2 + 1))
        a = jax.random.uniform(k3, (E2,), dtype=jnp.float32, minval=-limit, maxval=limit)
        bias = jnp.zeros((K, K), dtype=jnp.float32)
        return {'x': x, 'W': W, 'b_lin': b_lin, 'a': a, 'bias': bias}
    _L0_gnn_all = _L0_gnn_setup()
    _L0_gnn_in = {k: v for k, v in _L0_gnn_all.items() if k in ('b_lin', 'a', )}
    del _L0_gnn_all

    def _L1_gnn_setup():
        import jax, jax.numpy as jnp
        import numpy as np
        ALPHA = 0.005

        def _linear_init(key, fan_in, shape):
            bound = 1.0 / np.sqrt(fan_in)
            return jax.random.uniform(key, shape, jnp.float32, -bound, bound)
        key = jax.random.key(seed)
        ks = jax.random.split(key, 12)
        B, N, NI, NH, NO = (4, 512, 128, 128, 128)
        x = jax.random.normal(ks[0], (B, N, NI), jnp.float32)
        adj = (jax.random.uniform(ks[1], (N, N)) < 0.05).astype(jnp.float32)
        Wi = _linear_init(ks[2], NI, (NI, NH))
        bi = _linear_init(ks[3], NI, (NH,))
        We = _linear_init(ks[4], 2 * NH, (2 * NH, 1))
        be = _linear_init(ks[5], 2 * NH, (1,))
        Wn = _linear_init(ks[6], 2 * NH, (2 * NH, NO))
        bn = _linear_init(ks[7], 2 * NH, (NO,))
        Wm = _linear_init(ks[8], 2 * NH, (2 * NH, NO))
        bm = _linear_init(ks[9], 2 * NH, (NO,))
        return {'x': x, 'adj': adj, 'Wi': Wi, 'bi': bi, 'We': We, 'be': be, 'Wn': Wn, 'bn': bn, 'Wm': Wm, 'bm': bm}
    _L1_gnn_all = _L1_gnn_setup()
    _L1_gnn_in = {k: v for k, v in _L1_gnn_all.items() if k in ('Wi', 'bi', 'We', 'be', 'Wn', 'bn', 'Wm', 'bm', )}
    del _L1_gnn_all

    def _L2_gnn_setup():
        import jax, jax.numpy as jnp
        import numpy as np
        B, N, D = (4, 8192, 128)
        key = jax.random.key(seed)
        kx, ka, kq, kk, kv = jax.random.split(key, 5)
        x = jax.random.normal(kx, (B, N, D), dtype=jnp.float32)
        mask = (jax.random.uniform(ka, (N, N)) < 0.05).astype(jnp.float32)
        A_shape = jnp.clip(mask + jnp.eye(N, dtype=jnp.float32), 0.0, 1.0)
        q = jax.random.normal(kq, (D, D), dtype=jnp.float32)
        k = jax.random.normal(kk, (D, D), dtype=jnp.float32)
        v = jax.random.normal(kv, (D, D), dtype=jnp.float32)
        return {'x': x, 'A_shape': A_shape, 'q': q, 'k': k, 'v': v}
    _L2_gnn_all = _L2_gnn_setup()
    _L2_gnn_in = {k: v for k, v in _L2_gnn_all.items() if k in ('q', 'k', 'v', )}
    del _L2_gnn_all

    def _L3_gnn_setup():
        import jax, jax.numpy as jnp
        import numpy as np
        B, N, D = (32, 1024, 128)
        TIME_STEP = 5
        key = jax.random.key(seed)
        ks = jax.random.split(key, 12)
        s2 = 1.0 / np.sqrt(2 * D)
        s1 = 1.0 / np.sqrt(D)
        return {'input': jax.random.normal(ks[0], (B, N, D), jnp.float32), 'in_matrix': jax.random.uniform(ks[1], (N, N), jnp.float32), 'out_matrix': jax.random.uniform(ks[2], (N, N), jnp.float32), 'w3_w': jax.random.normal(ks[3], (D, 2 * D), jnp.float32) * s2, 'w3_b': jnp.zeros((D,), jnp.float32), 'u3_w': jax.random.normal(ks[4], (D, D), jnp.float32) * s1, 'u3_b': jnp.zeros((D,), jnp.float32), 'w4_w': jax.random.normal(ks[5], (D, 2 * D), jnp.float32) * s2, 'w4_b': jnp.zeros((D,), jnp.float32), 'w5_w': jax.random.normal(ks[6], (D, 2 * D), jnp.float32) * s2, 'w5_b': jnp.zeros((D,), jnp.float32), 'u5_w': jax.random.normal(ks[7], (D, D), jnp.float32) * s1, 'u5_b': jnp.zeros((D,), jnp.float32), 'time_step': TIME_STEP}
    _L3_gnn_all = _L3_gnn_setup()
    _L3_gnn_in = {k: v for k, v in _L3_gnn_all.items() if k in ('w3_w', 'w3_b', 'u3_w', 'u3_b', 'w4_w', 'w4_b', 'w5_w', 'w5_b', 'u5_w', 'u5_b', )}
    del _L3_gnn_all

    return {
        "x": x,
        "adj": adj,
        "L0_gnn_b_lin": _L0_gnn_in["b_lin"],
        "L0_gnn_a": _L0_gnn_in["a"],
        "L1_gnn_Wi": _L1_gnn_in["Wi"],
        "L1_gnn_bi": _L1_gnn_in["bi"],
        "L1_gnn_We": _L1_gnn_in["We"],
        "L1_gnn_be": _L1_gnn_in["be"],
        "L1_gnn_Wn": _L1_gnn_in["Wn"],
        "L1_gnn_bn": _L1_gnn_in["bn"],
        "L1_gnn_Wm": _L1_gnn_in["Wm"],
        "L1_gnn_bm": _L1_gnn_in["bm"],
        "L2_gnn_q": _L2_gnn_in["q"],
        "L2_gnn_k": _L2_gnn_in["k"],
        "L2_gnn_v": _L2_gnn_in["v"],
        "L3_gnn_w3_w": _L3_gnn_in["w3_w"],
        "L3_gnn_w3_b": _L3_gnn_in["w3_b"],
        "L3_gnn_u3_w": _L3_gnn_in["u3_w"],
        "L3_gnn_u3_b": _L3_gnn_in["u3_b"],
        "L3_gnn_w4_w": _L3_gnn_in["w4_w"],
        "L3_gnn_w4_b": _L3_gnn_in["w4_b"],
        "L3_gnn_w5_w": _L3_gnn_in["w5_w"],
        "L3_gnn_w5_b": _L3_gnn_in["w5_b"],
        "L3_gnn_u5_w": _L3_gnn_in["u5_w"],
        "L3_gnn_u5_b": _L3_gnn_in["u5_b"],
    }

def reference(x, adj, L0_gnn_b_lin, L0_gnn_a, L1_gnn_Wi, L1_gnn_bi, L1_gnn_We, L1_gnn_be, L1_gnn_Wn, L1_gnn_bn, L1_gnn_Wm, L1_gnn_bm, L2_gnn_q, L2_gnn_k, L2_gnn_v, L3_gnn_w3_w, L3_gnn_w3_b, L3_gnn_u3_w, L3_gnn_u3_b, L3_gnn_w4_w, L3_gnn_w4_b, L3_gnn_w5_w, L3_gnn_w5_b, L3_gnn_u5_w, L3_gnn_u5_b):
    import jax
    import jax.numpy as jnp
    def _L0_gnn_ref(x, W, b_lin, a, bias):
        import jax, jax.numpy as jnp
        import numpy as np
        ALPHA = 0.2
        F_DIM = 128
        F = x.shape[-1]
        W1, W2 = (W[:, :F], W[:, F:])
        s1 = jnp.einsum('bkf,ef->bke', x, W1)
        s2 = jnp.einsum('bkf,ef->bke', x, W2)
        pre = s1[:, :, None, :] + s2[:, None, :, :] + b_lin
        h = jnp.where(pre >= 0, pre, ALPHA * pre)
        e = jnp.einsum('bije,e->bij', h, a) + bias
        attn = jax.nn.softmax(e, axis=2)
        out = jax.nn.sigmoid(jnp.einsum('bij,bjf->bif', attn, x))
        return out

    def _L1_gnn_ref(x, adj, Wi, bi, We, be, Wn, bn, Wm, bm):
        import jax, jax.numpy as jnp
        import numpy as np
        ALPHA = 0.005

        def _linear_init(key, fan_in, shape):
            bound = 1.0 / np.sqrt(fan_in)
            return jax.random.uniform(key, shape, jnp.float32, -bound, bound)
        H = Wi.shape[1]
        x_h = jax.nn.elu(x @ Wi + bi)
        a_src = x_h @ We[:H, 0]
        a_tgt = x_h @ We[H:, 0]
        e = jax.nn.sigmoid(a_tgt[:, :, None] + a_src[:, None, :] + be[0])
        mask = adj + ALPHA * (1.0 - (adj != 0).astype(adj.dtype))
        e = e * mask
        agg = jnp.einsum('bij,bjh->bih', e, x_h)
        self_part = x_h * jnp.sum(e, axis=-1, keepdims=True)
        recv = jnp.concatenate([agg, self_part], axis=-1)
        recv = jax.nn.elu(recv @ Wn + bn)
        out = jnp.concatenate([recv, x_h], axis=-1) @ Wm + bm
        return out

    def _L2_gnn_ref(x, A_shape, q, k, v):
        import jax, jax.numpy as jnp
        import numpy as np
        B, N, D = (4, 8192, 128)
        input_dimension = x.shape[-1]
        Q = x @ q
        K = x @ k
        A = jnp.einsum('bnd,bmd->bnm', Q, K)
        A = A / jnp.sqrt(jnp.float32(input_dimension))
        A = jnp.tanh(A / 8.0) * 8.0
        A = jnp.exp(A) * A_shape
        A = A / jnp.sum(A, axis=-1, keepdims=True)
        out = A @ x @ v
        return out

    def _L3_gnn_ref(input, in_matrix, out_matrix, w3_w, w3_b, u3_w, u3_b, w4_w, w4_b, w5_w, w5_b, u5_w, u5_b, time_step):
        import jax, jax.numpy as jnp
        import numpy as np
        B, N, D = (32, 1024, 128)
        TIME_STEP = 5
        def step(h, _):
            m_in = jnp.einsum('nm,bmd->bnd', in_matrix, h)
            m_out = jnp.einsum('nm,bmd->bnd', out_matrix, h)
            av = jnp.concatenate([m_in, m_out], axis=-1)
            u3 = h @ u3_w.T + u3_b
            z = jax.nn.sigmoid(av @ w3_w.T + w3_b + u3)
            r = jax.nn.sigmoid(av @ w4_w.T + w4_b + u3)
            hv = jnp.tanh(av @ w5_w.T + w5_b + (r * h @ u5_w.T + u5_b))
            h = (1.0 - z) * h + z * hv
            return (h, None)
        h, _ = jax.lax.scan(step, input, None, length=time_step)
        return h

    h = jnp.maximum(_layernorm(x, axis=-1), 0.0)
    x = x + _L0_gnn_ref(h, adj, L0_gnn_b_lin, L0_gnn_a, adj)
    h = jnp.maximum(_layernorm(x, axis=-1), 0.0)
    x = x + _L1_gnn_ref(h, adj, L1_gnn_Wi, L1_gnn_bi, L1_gnn_We, L1_gnn_be, L1_gnn_Wn, L1_gnn_bn, L1_gnn_Wm, L1_gnn_bm)
    h = jnp.maximum(_layernorm(x, axis=-1), 0.0)
    x = x + _L2_gnn_ref(h, adj, L2_gnn_q, L2_gnn_k, L2_gnn_v)
    h = jnp.maximum(_layernorm(x, axis=-1), 0.0)
    x = x + _L3_gnn_ref(h, adj, adj, L3_gnn_w3_w, L3_gnn_w3_b, L3_gnn_u3_w, L3_gnn_u3_b, L3_gnn_w4_w, L3_gnn_w4_b, L3_gnn_w5_w, L3_gnn_w5_b, L3_gnn_u5_w, L3_gnn_u5_b, 5)
    return x


_drawn_inputs = setup_inputs


def setup_inputs(seed=0):
    import zlib

    import numpy as np

    out = dict(_drawn_inputs(seed))
    spreads = {'L0_gnn_b_lin': (0.0, 2.0),
     'L3_gnn_w3_b': (0.0, 0.8),
     'L3_gnn_u3_b': (0.0, 0.8),
     'L3_gnn_w4_b': (0.0, 2.0),
     'L3_gnn_w5_b': (0.0, 0.453),
     'L3_gnn_u5_b': (0.0, 0.448)}
    factors = {'L0_gnn_a': 4.663, 'L1_gnn_We': 4.142, 'L3_gnn_w4_w': 4.033}
    for name, (base, spread) in spreads.items():
        noise = np.random.default_rng([zlib.crc32(name.encode()), seed]).standard_normal(out[name].shape)
        drawn = base * np.exp(spread * noise) if base else spread * noise
        out[name] = jnp.asarray(drawn.astype(out[name].dtype))
    for name, factor in factors.items():
        out[name] = (out[name] * factor).astype(out[name].dtype)
    return out
```

```python
from contextlib import ExitStack

import concourse.bass as bass
from concourse import mybir

F32 = mybir.dt.float32
ALU = mybir.AluOpType
ACT = mybir.ActivationFunctionType
AXIS = mybir.AxisListType

P = 128
N = 256
NB = N // P
E = 256
EC = E // P
NEG_SLOPE0 = 0.2
MASK_ALPHA1 = 0.005
LN_EPS = 1e-5
STEPS = 5
LOGIT_BOUND2 = 8.0

GROUPS = 4
ROWS = P // GROUPS
LOTS_B = EC * ROWS
LOTS = 2 * LOTS_B
BLOCKS = GROUPS * NB
RING = 8
ROUNDS = LOTS // RING

LEAD = 4
POST = dict(score=5, exp=6, transpose=8, copy=9, aggregate=10, tanh=11, residual=12)
PRE = dict(stats=38, norm=41, transpose=44, copy=45, project=47, evacuate=49)
LN1 = dict(stats=13, norm=14, transpose=16, copy=17)
L1 = dict(project=18, exp=19, elu=20, edge_terms=22, edge_copy=23, tanh=24, mask=25, aggregate=27, agg_copy=28,
          receive=29, recv_exp=30, recv_elu=31, out=33, residual=34)
LN2 = dict(stats=35, norm=36, transpose=38, copy=39)
L2 = dict(project=40, copy=41, scores=42, tanh=43, exp=44, mask=45, aggregate=47, residual=48)
LN3 = dict(stats=49, norm=50, transpose=53, copy=54)
L3_AT, L3_PERIOD = 55, 14
L3 = dict(message=0, copy=1, gates=2, reset=4, update=5, candidate=7, tanh=8, state=9, transpose=11, back=12)

LOADS_COUNT = 24
DVE_CONST_TURNED, DVE_CONST_ALL = 10, 12

VECTOR_BLOCK, SCALAR_BLOCK = 2.63, 4.0


def stage_costs():
    vector, scalar = [0.0] * LOTS, [0.0] * LOTS

    def put(costs, table, at, **stages):
        for name, cost in stages.items():
            costs[at + table[name]] += cost

    for half in (0, LOTS_B):
        put(vector, POST, half, score=13.9, transpose=1.5, residual=3.4)
        put(scalar, POST, half, exp=10, copy=4.8, tanh=5)
        put(vector, PRE, half, stats=7.5, norm=6, evacuate=8.5)
        put(scalar, PRE, half, copy=2.6, evacuate=4.8)
    for ln, stats, norm in ((LN1, 17, 8), (LN2, 11, 8), (LN3, 11, 11.4)):
        put(vector, ln, 0, stats=stats, norm=norm)
        put(scalar, ln, 0, copy=4.8)
    put(vector, L1, 0, elu=10, edge_copy=1.3, mask=12, agg_copy=6, recv_elu=10, residual=6)
    put(scalar, L1, 0, exp=5.7, edge_copy=4.8, tanh=14.2, agg_copy=4.8, recv_exp=5.7)
    put(vector, L2, 0, copy=6, mask=11.4, residual=11.8)
    put(scalar, L2, 0, copy=4.8, tanh=9.6, exp=9.5)
    for s in range(STEPS):
        put(vector, L3, L3_AT + s * L3_PERIOD, update=6, state=18)
        put(scalar, L3, L3_AT + s * L3_PERIOD, copy=4.8, reset=5.7, update=5.7, tanh=5.7, back=4.8 if s < STEPS - 1 else 0)
    return vector, scalar


def share_blocks():
    vector, scalar = stage_costs()
    shares, v, s = [], 0.0, 0.0
    for t in range(LOTS):
        n = min(range(1, BLOCKS), key=lambda n: max(v + (BLOCKS - n) * VECTOR_BLOCK, s + n * SCALAR_BLOCK))
        shares.append(n)
        v += (BLOCKS - n) * VECTOR_BLOCK + vector[t]
        s += n * SCALAR_BLOCK + scalar[t]
    return shares


ACT_BLOCKS = share_blocks()


def gnn_stack(nc, x, adj, L0_b, L0_a, L1_Wi, L1_bi, L1_We, L1_be, L1_Wn, L1_bn, L1_Wm, L1_bm, L2_q, L2_k, L2_v,
              L3_w3_w, L3_w3_b, L3_u3_w, L3_u3_b, L3_w4_w, L3_w4_b, L3_w5_w, L3_w5_b, L3_u5_w, L3_u5_b, out):
    BATCHES = x.shape[0]
    PAIRS = BATCHES // 2
    x_rows = x.rearrange("b (r p) d -> b p r d", p=P)
    out_rows = out.rearrange("b (r p) d -> b p r d", p=P)

    class Turn:

        def __init__(self, m=None, it=None):
            self.m, self.it = m, it
            self.has_main = it is not None or m < PAIRS
            self.has_rest = it is not None or m >= 1
            self.pre_next = it is not None or m < PAIRS - 1

        def at(self, per_turn, more):
            if self.it is None:
                return per_turn * self.m + more
            return self.it * per_turn + (per_turn + more)

    def need(eng, sem, value):
        if isinstance(value, int) and value <= 0:
            return
        eng.wait_ge(sem, value)

    def run_turns(eng, body):
        body(Turn(m=0))
        with eng.Fori(0, PAIRS - 2) as it:
            body(Turn(it=it))
        body(Turn(m=PAIRS - 1))
        body(Turn(m=PAIRS))

    def halves(turn):
        return [(y * LOTS_B, y) for y in range(2)]

    with ExitStack() as ctx:
        def sb(name, shape):
            return ctx.enter_context(nc.sbuf_tensor(name, shape, F32))

        def bank(name):
            return ctx.enter_context(nc.psum_tensor(name, [P, 512], F32))

        def sem(name):
            return ctx.enter_context(nc.semaphore(name))

        ident = sb("ident", [P, P])
        ones = sb("ones", [P, P])
        eps = sb("eps", [P, 4])
        minus_half = sb("minus_half", [P, 4])
        A = sb("A", [P, NB, N])
        AT = sb("AT", [P, NB, N])
        a_col = sb("a_col", [P, EC])
        a_lin = sb("a_lin", [P, EC])
        a_lin_wide = sb("a_lin_wide", [P, EC, P])
        a_window = sb("a_window", [P, EC, 2 * ROWS - 1])
        b0_col = sb("b0_col", [P, EC])
        w_lin = sb("w_lin", [P, 3])
        w2_lin_wide = sb("w2_lin_wide", [P, P])
        A_bias = sb("A_bias", [P, NB, N])
        maskT = sb("maskT", [P, NB, N])
        maskT_tmp = sb("maskT_tmp", [P, NB, N])
        Wi = sb("Wi", [P, P])
        We = sb("We", [P, 2])
        be = sb("be", [P, 1])
        We_tgt_wide = sb("We_tgt_wide", [P, P])
        Wn = sb("Wn", [P, 2, P])
        Wm = sb("Wm", [P, 2, P])
        bm_wide = sb("bm_wide", [P, P])
        cols = sb("cols", [P, 7])
        bias3 = sb("bias3", [P, 3])
        raw2 = sb("raw2", [P, 2, P])
        Wv = sb("Wv", [P, P])
        raw3 = sb("raw3", [P, 3, 2 * P])
        rawu = sb("rawu", [P, 2, P])
        turned = sb("turned", [P, 4, P])
        G = sb("G", [P, P])
        W345 = sb("W345", [P, 3, P])
        qT, kT, u3T, u5T_half = (turned[:, n, :] for n in range(4))

        X0 = sb("X0", [P, 2, NB, P])
        X0_half = sb("X0_half", [P, 2, NB, P])
        H0 = sb("H0", [P, 2, NB, P])
        H0T = sb("H0T", [P, 2, N])
        U = sb("U", [P, 2, EC, N])
        V = sb("V", [P, 2, EC, N])
        lin_i = sb("lin_i", [P, 2, NB])
        ring = sb("ring", [P, RING, GROUPS, NB * N])
        st0 = sb("st0", [P, NB, 6])
        mv0 = sb("mv0", [P, NB, 2])
        var0 = sb("var0", [P, NB])
        rstd0 = sb("rstd0", [P, NB])
        normed0 = sb("normed0", [P, NB, P])
        score = sb("score", [P, NB, N])
        prob = sb("prob", [P, NB, N])
        probT = sb("probT", [P, NB, N])
        neg_max = sb("neg_max", [P, NB])
        row_sum = sb("row_sum", [P, NB])
        inv_sum = sb("inv_sum", [P, NB])
        half_inv = sb("half_inv", [P, NB])
        tanh0 = sb("tanh0", [P, NB, P])

        X1 = sb("X1", [P, 4, P])
        X1_bm = sb("X1_bm", [P, 4, P])
        X2 = sb("X2", [P, 4, P])
        X3 = sb("X3", [P, 4, P])
        OUT = sb("OUT", [P, 4, P])
        st = sb("st", [P, 3, 4, 6])
        wait_carrier = sb("wait_carrier", [P, 1])
        mv = sb("mv", [P, 3, 4, 2])
        var = sb("var", [P, 3, 4])
        rstd = sb("rstd", [P, 3, 4])
        normed = sb("normed", [P, 3, 4, P])
        h1T = sb("h1T", [P, 2 * N])
        exp1 = sb("exp1", [P, 2 * N])
        xhT = sb("xhT", [P, 2 * N])
        xh = sb("xh", [P, 4, P])
        src_bias = sb("src_bias", [P, 4])
        edge = sb("edge", [P, 2, NB, N])
        aggT = sb("aggT", [P, 2 * N])
        selfT = sb("selfT", [P, 2 * N])
        exp1r = sb("exp1r", [P, 2 * N])
        recvT = sb("recvT", [P, 2 * N])
        h2T = sb("h2T", [P, 2 * N])
        YT = sb("YT", [P, 2 * N])
        HV = sb("HV", [P, 4, P + 1])
        logit2 = sb("logit2", [P, 2, NB, N])
        weight2 = sb("weight2", [P, 2, NB, N])
        inv2 = sb("inv2", [P, 4])
        h3T = sb("h3T", [P, 2 * N])
        h3 = sb("h3", [P, 4, P])
        mT = sb("mT", [P, 2 * N])
        tr = sb("tr", [P, 2 * N])
        tz = sb("tz", [P, 2 * N])
        rh = sb("rh", [P, 2 * N])
        cand = sb("cand", [P, 2 * N])
        diff = sb("diff", [P, 2 * N])
        gated = sb("gated", [P, 2 * N])

        S = [bank("S0"), bank("S1")]
        PA, PB, PC = bank("PA"), bank("PB"), bank("PC")
        R0, R1, R2 = bank("R0"), bank("R1"), bank("R2")

        loaded = sem("loaded")
        gp_const, dve_const, pe_const = sem("gp_const"), sem("dve_const"), sem("pe_const")
        by_dve = [sem(f"by_dve{n}") for n in range(RING)]
        by_act = [sem(f"by_act{n}") for n in range(RING)]
        freed = [sem(f"freed{n}") for n in range(RING)]
        x_loaded, pre_stats, pre_mv, pre_eps, pre_rstd = (sem(n) for n in "x_loaded pre_stats pre_mv pre_eps pre_rstd".split())
        pre_normed, h0_ready, h0T_psum, h0T_ready = (sem(n) for n in "pre_normed h0_ready h0T_psum h0T_ready".split())
        uv_psum, u_ready, v_ready = (sem(n) for n in "uv_psum u_ready v_ready".split())
        score_ready, max_ready, prob_ready = (sem(n) for n in "score_ready max_ready prob_ready".split())
        probT_psum, probT_ready, inv_ready, half_inv_ready = (sem(n) for n in "probT_psum probT_ready inv_ready half_inv_ready".split())
        attn_psum, tanh0_ready, x1_ready = (sem(n) for n in "attn_psum tanh0_ready x1_ready".split())
        ln_stats = [sem(f"ln{n}_stats") for n in (1, 2, 3)]
        ln_mv = [sem(f"ln{n}_mv") for n in (1, 2, 3)]
        ln_eps = [sem(f"ln{n}_eps") for n in (1, 2, 3)]
        ln_rstd = [sem(f"ln{n}_rstd") for n in (1, 2, 3)]
        ln_normed = [sem(f"ln{n}_normed") for n in (1, 2, 3)]
        hT_psum = [sem(f"h{n}T_psum") for n in (1, 2, 3)]
        hT_ready = [sem(f"h{n}T_ready") for n in (1, 2, 3)]
        x1bm_ready = sem("x1bm_ready")
        xh_psum, xh_exp, xh_min, xhT_ready = (sem(n) for n in "xh_psum xh_exp xh_min xhT_ready".split())
        edge_psum, src_ready, xh_ready, edge_tanh, edge_ready = (sem(n) for n in "edge_psum src_ready xh_ready edge_tanh edge_ready".split())
        agg1_psum, aggT_ready, selfT_ready = (sem(n) for n in "agg1_psum aggT_ready selfT_ready".split())
        recv_psum, recv_exp, recv_min, recvT_ready = (sem(n) for n in "recv_psum recv_exp recv_min recvT_ready".split())
        out1_psum, x2_ready = sem("out1_psum"), sem("x2_ready")
        y_psum, yT_ready, hv_ready, logit_psum, tanh2_ready = (sem(n) for n in "y_psum yT_ready hv_ready logit_psum tanh2_ready".split())
        exp2_ready, weight2_ready, agg2_psum, inv2_ready, x3_ready = (sem(n) for n in "exp2_ready weight2_ready agg2_psum inv2_ready x3_ready".split())
        h3_ready = sem("h3_ready")
        m_psum, mT_ready, gates_psum, tr_ready, tz_ready, rh_ready = (sem(n) for n in "m_psum mT_ready gates_psum tr_ready tz_ready rh_ready".split())
        cand_psum, cand_ready, diff_ready, gated_ready = (sem(n) for n in "cand_psum cand_ready diff_ready gated_ready".split())
        state_ready, state_psum, state_back = (sem(n) for n in "state_ready state_psum state_back".split())
        out_ready, out_stored = sem("out_ready"), sem("out_stored")

        block = ctx.enter_context(nc.Block())

        @block.sync
        def _(sp):
            def load(dst, src):
                sp.dma_start(dst, src, allow_slow_non_contiguous=True).then_inc(loaded, 16)
                count[0] += 1

            count = [0]
            sp.sem_inc(out_stored, 16)
            sp.dma_start(X0[:, 0], x_rows[0]).then_inc(x_loaded, 16)
            load(A[:], adj.rearrange("(r p) j -> p r j", p=P))
            load(a_col[:], L0_a.rearrange("(c p) -> p c", p=P))
            load(b0_col[:], L0_b.rearrange("(c p) -> p c", p=P))
            load(Wi[:], L1_Wi)
            load(We[:], L1_We.rearrange("(c p) o -> p (c o)", p=P))
            load(be[:], L1_be.partition_broadcast(P))
            load(Wn[:], L1_Wn.rearrange("(c p) o -> p c o", p=P))
            load(Wm[:], L1_Wm.rearrange("(c p) o -> p c o", p=P))
            load(bm_wide[:], L1_bm.partition_broadcast(P))
            for n, b in enumerate((L1_bi, L1_bn, L3_w3_b, L3_w4_b, L3_w5_b, L3_u3_b, L3_u5_b)):
                load(cols[:, n:n + 1], b.rearrange("(p o) -> p o", o=1))
            load(raw2[:, 0], L2_q)
            load(raw2[:, 1], L2_k)
            load(Wv[:], L2_v)
            for n, w in enumerate((L3_w3_w, L3_w4_w, L3_w5_w)):
                load(raw3[:, n], w)
            load(rawu[:, 0], L3_u3_w)
            load(rawu[:, 1], L3_u5_w)
            assert count[0] == LOADS_COUNT, count

            def body(turn):
                for y in range(2):
                    if turn.has_main and (y == 0 or turn.pre_next):
                        need(sp, x1_ready, turn.at(2, y))
                        b = turn.at(2, y + 1)
                        sp.dma_start(X0[:, 1 - y], x_rows[b] if isinstance(b, int) else x_rows[bass.ds(b, 1)].rearrange("o p r d -> (o p) r d")).then_inc(x_loaded, 16)
                if turn.has_rest:
                    need(sp, out_ready, turn.at(1, 0))
                    for y in range(2):
                        b = turn.at(2, y - 2)
                        dst = out_rows[b] if isinstance(b, int) else out_rows[bass.ds(b, 1)].rearrange("o p r d -> (o p) r d")
                        sp.dma_start(dst, OUT[:, NB * y:NB * y + NB]).then_inc(out_stored, 16)

            run_turns(sp, body)
            sp.wait_ge(out_stored, 16 * (BATCHES + 1))

        @block.gpsimd
        def _(gp):
            gp.memset(ident[:], 0.0).then_inc(gp_const, 1)
            gp.wait_ge(gp_const, 1)
            gp.affine_select(out=ident[:], in_=ident[:], compare_op=ALU.not_equal, fill=1.0, base=0,
                             pattern=[[-1, P]], channel_multiplier=1).then_inc(gp_const, 1)
            gp.wait_ge(dve_const, 1)

            def inverse_root(mean_var, tmp, dst, width, sem_in, sem_eps, sem_out, value):
                gp.wait_ge(sem_in, value)
                gp.tensor_tensor(tmp, mean_var, eps[:, 0:width], ALU.add).then_inc(sem_eps, 1)
                gp.wait_ge(sem_eps, value)
                gp.tensor_tensor(dst, tmp, minus_half[:, 0:width], ALU.pow).then_inc(sem_out, 1)

            def pre(value):
                inverse_root(mv0[:, :, 1], var0[:], rstd0[:], NB, pre_mv, pre_eps, pre_rstd, value)

            def norm(n, turn):
                inverse_root(mv[:, n, :, 1], var[:, n], rstd[:, n], 4, ln_mv[n], ln_eps[n], ln_rstd[n], turn.at(1, 0))

            pre(1)

            def body(turn):
                for t in range(LOTS):
                    y, p = divmod(t, LOTS_B)
                    if p == PRE["stats"] and turn.has_main and (y == 0 or turn.pre_next):
                        pre(turn.at(2, y + 2))
                    if turn.has_rest:
                        for n, ln in enumerate((LN1, LN2, LN3)):
                            if t == ln["stats"]:
                                norm(n, turn)

            run_turns(gp, body)

        @block.vector
        def _(dve):
            chain = [1]

            def constant(ins):
                chain[0] += 1
                ins.then_inc(dve_const, 1)
                dve.wait_ge(dve_const, chain[0])

            dve.memset(eps[:], LN_EPS)
            dve.memset(minus_half[:], -0.5).then_inc(dve_const, 1)
            dve.memset(ones[:], 1.0)
            dve.memset(HV[:, :, P:P + 1], 1.0)
            constant(dve.memset(a_window[:], 0.0))
            dve.wait_ge(loaded, 16 * LOADS_COUNT)
            dve.tensor_scalar(a_window[:, :, ROWS - 1:ROWS], a_col[:].unsqueeze(2), 1.0 - NEG_SLOPE0, None, ALU.mult)
            constant(dve.tensor_scalar(a_lin[:], a_col[:], NEG_SLOPE0, None, ALU.mult))
            dve.tensor_copy(We_tgt_wide[:], We[:, 1:2].to_broadcast([P, P]))
            dve.tensor_tensor(bias3[:, 0:2], cols[:, 2:4], cols[:, 5:6].to_broadcast([P, 2]), ALU.add)
            dve.tensor_tensor(bias3[:, 2:3], cols[:, 4:5], cols[:, 6:7], ALU.add)
            constant(dve.tensor_copy(a_lin_wide[:], a_lin[:].unsqueeze(2).to_broadcast([P, EC, P])))
            constant(dve.tensor_scalar(bias3[:, 0:2], bias3[:, 0:2], 0.5, None, ALU.mult))
            dve.wait_ge(pe_const, 1)
            constant(dve.tensor_copy(AT[:], R0[:].rearrange("p (r i) -> p r i", r=NB)))
            constant(dve.tensor_scalar(maskT_tmp[:], AT[:], 0.0, -0.5 * MASK_ALPHA1, ALU.not_equal, ALU.mult))
            constant(dve.tensor_scalar(maskT_tmp[:], maskT_tmp[:], 0.5 * MASK_ALPHA1, None, ALU.add))
            constant(dve.scalar_tensor_tensor(maskT[:], AT[:], 0.5, maskT_tmp[:], ALU.mult, ALU.add))
            dve.wait_ge(pe_const, 2)
            dve.tensor_copy(turned[:, 0:3], R1[:, 0:3 * P].rearrange("p (n k) -> p n k", n=3))
            dve.tensor_scalar(turned[:, 3], R1[:, 3 * P:4 * P], 0.5, None, ALU.mult)
            constant(dve.tensor_copy(W345[:], R2[:, 0:3 * P].rearrange("p (n k) -> p n k", n=3)))
            at_const_ready = chain[0]
            dve.wait_ge(pe_const, 3)
            dve.tensor_copy(G[:], PB[:, 0:P])
            constant(dve.tensor_copy(w_lin[:], PC[:, 0:3]))
            dve.tensor_copy(w2_lin_wide[:], w_lin[:, 1:2].to_broadcast([P, P]))
            constant(dve.tensor_scalar(A_bias[:], A[:], w_lin[:, 2:3], None, ALU.add))
            assert (at_const_ready, chain[0]) == (DVE_CONST_TURNED, DVE_CONST_ALL), (at_const_ready, chain[0])

            def blocks(turn, t):
                y, p = divmod(t, LOTS_B)
                row, c = divmod(p, EC)
                place, rnd = t % RING, t // RING
                need(dve, freed[place], turn.at(ROUNDS, rnd))
                if p == 0:
                    dve.wait_ge(u_ready, turn.at(2, y + 1))
                    dve.wait_ge(v_ready, turn.at(2, y + 1))
                for n in range(BLOCKS - ACT_BLOCKS[t]):
                    g, half = divmod(n, NB)
                    i = half * P + g * ROWS + row
                    last = dve.tensor_scalar(ring[:, place, g, half * N:(half + 1) * N], V[:, y, c],
                                             U[:, y, c, i:i + 1], 0.0, ALU.add, ALU.max)
                last.then_inc(by_dve[place], 1)

            def pre(p, y, value):
                if p == PRE["stats"]:
                    dve.wait_ge(x_loaded, value * 16)
                    for r in range(NB):
                        last = dve.bn_stats(st0[:, r], X0[:, y, r])
                    last.then_inc(pre_stats, 1)
                    dve.wait_ge(pre_stats, value)
                    dve.tensor_scalar(X0_half[:, y], X0[:, y], 0.5, None, ALU.add)
                    for r in range(NB):
                        last = dve.bn_aggr(mv0[:, r], st0[:, r])
                    last.then_inc(pre_mv, 1)
                if p == PRE["norm"]:
                    dve.wait_ge(pre_rstd, value)
                    for r in range(NB):
                        last = dve.tensor_scalar(normed0[:, r], X0[:, y, r], mv0[:, r, 0:1], rstd0[:, r:r + 1],
                                                 ALU.subtract, ALU.mult)
                    last.then_inc(pre_normed, 1)
                    dve.wait_ge(pre_normed, value)
                    dve.tensor_scalar(H0[:, y], normed0[:], 0.0, None, ALU.max).then_inc(h0_ready, 1)
                if p == PRE["evacuate"]:
                    dve.wait_ge(uv_psum, value)
                    dve.tensor_copy(lin_i[:, y], PA[:, N:N + NB])
                    for c in range(EC):
                        last = dve.tensor_scalar(V[:, y, c], PC[:, c * N:(c + 1) * N], b0_col[:, c:c + 1], None, ALU.add)
                    last.then_inc(v_ready, 1)

            def post(p, y, value, lots_done):
                if p == POST["score"]:
                    dve.wait_ge(freed[RING - 1], lots_done)
                    for r in range(NB):
                        last = dve.scalar_tensor_tensor(score[:, r], S[y][:, r * N:(r + 1) * N], lin_i[:, y, r:r + 1],
                                                        A_bias[:, r], ALU.add, ALU.add)
                    last.then_inc(score_ready, 1)
                    dve.wait_ge(score_ready, value)
                    dve.tensor_reduce(neg_max[:], score[:], AXIS.X, ALU.max, negate=True).then_inc(max_ready, 1)
                if p == POST["transpose"]:
                    dve.wait_ge(prob_ready, value)
                    dve.reciprocal(inv_sum[:], row_sum[:]).then_inc(inv_ready, 1)
                    dve.wait_ge(inv_ready, value)
                    dve.tensor_scalar(half_inv[:], inv_sum[:], 0.5, None, ALU.mult).then_inc(half_inv_ready, 1)
                if p == POST["residual"]:
                    dve.wait_ge(tanh0_ready, value)
                    dve.scalar_tensor_tensor(X1[:, NB * y:NB * y + NB], tanh0[:], 0.5, X0_half[:, y], ALU.mult,
                                             ALU.add).then_inc(x1_ready, 1)

            def norm(t, ln, n, src, turn):
                if t == ln["stats"]:
                    for r in range(4):
                        last = dve.bn_stats(st[:, n, r], src[:, r])
                    last.then_inc(ln_stats[n], 1)
                    dve.wait_ge(ln_stats[n], turn.at(1, 0))
                    if n == 0:
                        dve.tensor_tensor(X1_bm[:], X1[:], bm_wide[:].unsqueeze(1).to_broadcast([P, 4, P]),
                                          ALU.add).then_inc(x1bm_ready, 1)
                    else:
                        dve.memset(wait_carrier[:], 0.0)
                    for r in range(4):
                        last = dve.bn_aggr(mv[:, n, r], st[:, n, r])
                    last.then_inc(ln_mv[n], 1)
                if t == ln["norm"]:
                    dve.wait_ge(ln_rstd[n], turn.at(1, 0))
                    for r in range(4):
                        last = dve.tensor_scalar(normed[:, n, r], src[:, r], mv[:, n, r, 0:1], rstd[:, n, r:r + 1],
                                                 ALU.subtract, ALU.mult)
                    last.then_inc(ln_normed[n], 1)

            def elu(bank_, bias, exp_, dst, sem_exp, sem_min, sem_out, turn):
                dve.wait_ge(sem_exp, turn.at(1, 0))
                dve.tensor_scalar(exp_[:], exp_[:], 1.0, 1.0, ALU.min, ALU.subtract).then_inc(sem_min, 1)
                dve.wait_ge(sem_min, turn.at(1, 0))
                dve.scalar_tensor_tensor(dst[:], bank_[:], bias, exp_[:], ALU.add, ALU.max).then_inc(sem_out, 1)

            def layer1(t, turn):
                pair = turn.at(1, 0)
                if t == LN1["stats"]:
                    dve.wait_ge(x1_ready, turn.at(2, 0))
                norm(t, LN1, 0, X1, turn)
                if t == L1["elu"]:
                    elu(R1, cols[:, 0:1], exp1, xhT, xh_exp, xh_min, xhT_ready, turn)
                if t == L1["edge_copy"]:
                    dve.wait_ge(edge_psum, pair)
                    dve.tensor_scalar(src_bias[:], R1[:, 0:4], be[:], 0.5, ALU.add, ALU.mult).then_inc(src_ready, 1)
                if t == L1["mask"]:
                    dve.wait_ge(edge_tanh, pair)
                    for y in range(2):
                        last = dve.scalar_tensor_tensor(edge[:, y], edge[:, y], 1.0, maskT[:], ALU.add, ALU.mult)
                    last.then_inc(edge_ready, 1)
                if t == L1["agg_copy"]:
                    dve.wait_ge(agg1_psum, pair)
                    dve.tensor_tensor(selfT[:], xhT[:], R0[:], ALU.mult).then_inc(selfT_ready, 1)
                if t == L1["recv_elu"]:
                    elu(R1, cols[:, 1:2], exp1r, recvT, recv_exp, recv_min, recvT_ready, turn)
                if t == L1["residual"]:
                    dve.wait_ge(out1_psum, pair)
                    dve.wait_ge(x1bm_ready, pair)
                    dve.tensor_tensor(X2[:], R0[:].rearrange("p (r d) -> p r d", r=4), X1_bm[:],
                                      ALU.add).then_inc(x2_ready, 1)

            def layer2(t, turn):
                pair = turn.at(1, 0)
                if t == LN2["stats"]:
                    dve.wait_ge(x2_ready, pair)
                norm(t, LN2, 1, X2, turn)
                if t == L2["copy"]:
                    dve.wait_ge(y_psum, pair)
                    dve.tensor_copy(HV[:, :, 0:P], R0[:].rearrange("p (r d) -> p r d", r=4)).then_inc(hv_ready, 1)
                if t == L2["mask"]:
                    dve.wait_ge(exp2_ready, pair)
                    dve.tensor_tensor(weight2[:], weight2[:], AT[:].unsqueeze(1).to_broadcast([P, 2, NB, N]),
                                      ALU.mult).then_inc(weight2_ready, 1)
                if t == L2["residual"]:
                    dve.wait_ge(agg2_psum, pair)
                    for y, bank_ in enumerate((R0, R1)):
                        sums = bank_[:, 0:NB * (P + 1)].rearrange("p (r d) -> p r d", r=NB)
                        last = dve.reciprocal(inv2[:, NB * y:NB * y + NB], sums[:, :, P])
                    last.then_inc(inv2_ready, 1)
                    dve.wait_ge(inv2_ready, pair)
                    for n in range(4):
                        bank_, r = (R0, R1)[n // NB], n % NB
                        last = dve.scalar_tensor_tensor(X3[:, n], bank_[:, r * (P + 1):r * (P + 1) + P], inv2[:, n:n + 1],
                                                        X2[:, n], ALU.mult, ALU.add)
                    last.then_inc(x3_ready, 1)

            def layer3(t, turn):
                pair = turn.at(1, 0)
                if t == LN3["stats"]:
                    dve.wait_ge(x3_ready, pair)
                norm(t, LN3, 2, X3, turn)
                if t == LN3["norm"]:
                    dve.wait_ge(ln_normed[2], pair)
                    dve.tensor_scalar(h3[:], normed[:, 2], 0.0, None, ALU.max).then_inc(h3_ready, 1)
                s, p = divmod(t - L3_AT, L3_PERIOD)
                if not 0 <= s < STEPS:
                    return
                step = turn.at(STEPS, s + 1 - STEPS)
                if p == L3["update"]:
                    dve.wait_ge(tr_ready, step)
                    dve.scalar_tensor_tensor(rh[:], tr[:], 1.0, h3T[:], ALU.add, ALU.mult).then_inc(rh_ready, 1)
                if p == L3["state"]:
                    dve.wait_ge(cand_ready, step)
                    dve.tensor_tensor(diff[:], cand[:], h3T[:], ALU.subtract).then_inc(diff_ready, 1)
                    dve.wait_ge(diff_ready, step)
                    dve.scalar_tensor_tensor(gated[:], tz[:], 1.0, diff[:], ALU.add, ALU.mult).then_inc(gated_ready, 1)
                    dve.wait_ge(gated_ready, step)
                    dve.scalar_tensor_tensor(h3T[:], gated[:], 0.5, h3T[:], ALU.mult, ALU.add).then_inc(state_ready, 1)
                if p == L3["back"] and s == STEPS - 1:
                    dve.wait_ge(state_psum, step)
                    dve.wait_ge(out_stored, turn.at(32, -16))
                    dve.tensor_tensor(OUT[:], R1[:].rearrange("p (r d) -> p r d", r=4), X3[:], ALU.add).then_inc(out_ready, 1)

            for p in sorted(PRE.values()):
                pre(p, 0, 1)

            def body(turn):
                for t in range(LOTS):
                    y, p = divmod(t, LOTS_B)
                    if turn.has_main:
                        blocks(turn, t)
                    if (y == 0 and turn.has_rest) or (y == 1 and turn.has_main):
                        post(p, 1 - y, turn.at(2, y), turn.at(ROUNDS, y * ROUNDS // 2))
                    if turn.has_main and (y == 0 or turn.pre_next):
                        pre(p, 1 - y, turn.at(2, y + 2))
                    if turn.has_rest:
                        layer1(t, turn)
                        layer2(t, turn)
                        layer3(t, turn)

            run_turns(dve, body)

        @block.scalar
        def _(act):
            def blocks(turn, t):
                y, p = divmod(t, LOTS_B)
                row, c = divmod(p, EC)
                place, rnd = t % RING, t // RING
                need(act, freed[place], turn.at(ROUNDS, rnd))
                if p == 0:
                    act.wait_ge(u_ready, turn.at(2, y + 1))
                    act.wait_ge(v_ready, turn.at(2, y + 1))
                for n in range(BLOCKS - ACT_BLOCKS[t], BLOCKS):
                    g, half = divmod(n, NB)
                    i = half * P + g * ROWS + row
                    last = act.activation(ring[:, place, g, half * N:(half + 1) * N], V[:, y, c], ACT.Relu,
                                          bias=U[:, y, c, i:i + 1])
                last.then_inc(by_act[place], 1)

            def pre(p, y, value):
                if p == PRE["copy"]:
                    act.wait_ge(h0T_psum, value)
                    act.activation(H0T[:, y], PA[:, 0:N], ACT.Copy).then_inc(h0T_ready, 1)
                if p == PRE["evacuate"]:
                    act.wait_ge(uv_psum, value)
                    act.activation(U[:, y], PB[:].rearrange("p (c n) -> p c n", c=EC), ACT.Copy).then_inc(u_ready, 1)

            def post(p, y, value):
                if p == POST["exp"]:
                    act.wait_ge(max_ready, value)
                    for r in range(NB):
                        last = act.activation(prob[:, r], score[:, r], ACT.Exp, bias=neg_max[:, r:r + 1],
                                              accum_out=row_sum[:, r:r + 1])
                    last.then_inc(prob_ready, 1)
                if p == POST["copy"]:
                    act.wait_ge(probT_psum, value)
                    act.activation(probT[:], PB[:].rearrange("p (r i) -> p r i", r=NB), ACT.Copy).then_inc(probT_ready, 1)
                if p == POST["tanh"]:
                    act.wait_ge(attn_psum, value)
                    act.wait_ge(half_inv_ready, value)
                    for r in range(NB):
                        last = act.activation(tanh0[:, r], PC[:, r * P:(r + 1) * P], ACT.Tanh, scale=half_inv[:, r:r + 1])
                    last.then_inc(tanh0_ready, 1)

            def layer1(t, turn):
                pair = turn.at(1, 0)
                if t == LN1["copy"]:
                    act.wait_ge(hT_psum[0], pair)
                    act.activation(h1T[:], R0[:], ACT.Relu).then_inc(hT_ready[0], 1)
                if t == L1["exp"]:
                    act.wait_ge(xh_psum, pair)
                    act.activation(exp1[:], R1[:], ACT.Exp, bias=cols[:, 0:1]).then_inc(xh_exp, 1)
                if t == L1["edge_copy"]:
                    act.wait_ge(edge_psum, pair)
                    act.activation(xh[:], R2[:].rearrange("p (r d) -> p r d", r=4), ACT.Copy).then_inc(xh_ready, 1)
                if t == L1["tanh"]:
                    act.wait_ge(src_ready, pair)
                    for y in range(2):
                        for r in range(NB):
                            n = NB * y + r
                            last = act.activation(edge[:, y, r], R0[:, y * N:(y + 1) * N], ACT.Tanh,
                                                  bias=src_bias[:, n:n + 1], scale=0.5)
                    last.then_inc(edge_tanh, 1)
                if t == L1["agg_copy"]:
                    act.wait_ge(agg1_psum, pair)
                    act.activation(aggT[:], R2[:], ACT.Copy).then_inc(aggT_ready, 1)
                if t == L1["recv_exp"]:
                    act.wait_ge(recv_psum, pair)
                    act.activation(exp1r[:], R1[:], ACT.Exp, bias=cols[:, 1:2]).then_inc(recv_exp, 1)

            def layer2(t, turn):
                pair = turn.at(1, 0)
                if t == LN2["copy"]:
                    act.wait_ge(hT_psum[1], pair)
                    act.activation(h2T[:], R1[:], ACT.Relu).then_inc(hT_ready[1], 1)
                if t == L2["copy"]:
                    act.wait_ge(y_psum, pair)
                    act.activation(YT[:], R2[:], ACT.Copy).then_inc(yT_ready, 1)
                if t == L2["tanh"]:
                    act.wait_ge(logit_psum, pair)
                    for y, bank_ in enumerate((R1, R2)):
                        last = act.activation(logit2[:, y], bank_[:].rearrange("p (r n) -> p r n", r=NB), ACT.Tanh,
                                              scale=float(P) ** -0.5 / LOGIT_BOUND2)
                    last.then_inc(tanh2_ready, 1)
                if t == L2["exp"]:
                    act.wait_ge(tanh2_ready, pair)
                    act.activation(weight2[:], logit2[:], ACT.Exp, scale=LOGIT_BOUND2).then_inc(exp2_ready, 1)

            def layer3(t, turn):
                pair = turn.at(1, 0)
                if t == LN3["copy"]:
                    act.wait_ge(hT_psum[2], pair)
                    act.activation(h3T[:], R2[:], ACT.Copy).then_inc(hT_ready[2], 1)
                s, p = divmod(t - L3_AT, L3_PERIOD)
                if not 0 <= s < STEPS:
                    return
                step = turn.at(STEPS, s + 1 - STEPS)
                if p == L3["copy"]:
                    act.wait_ge(m_psum, step)
                    act.activation(mT[:], R0[:], ACT.Copy).then_inc(mT_ready, 1)
                if p == L3["reset"]:
                    act.wait_ge(gates_psum, step)
                    act.activation(tr[:], R2[:], ACT.Tanh, bias=bias3[:, 1:2], scale=0.5).then_inc(tr_ready, 1)
                if p == L3["update"]:
                    act.activation(tz[:], R1[:], ACT.Tanh, bias=bias3[:, 0:1], scale=0.5).then_inc(tz_ready, 1)
                if p == L3["tanh"]:
                    act.wait_ge(cand_psum, step)
                    act.activation(cand[:], R0[:], ACT.Tanh, bias=bias3[:, 2:3]).then_inc(cand_ready, 1)
                if p == L3["back"] and s < STEPS - 1:
                    act.wait_ge(state_psum, step)
                    act.activation(h3[:], R1[:].rearrange("p (r d) -> p r d", r=4), ACT.Copy).then_inc(state_back, 1)

            act.wait_ge(dve_const, DVE_CONST_ALL)
            for p in sorted(PRE.values()):
                pre(p, 0, 1)

            def body(turn):
                for t in range(LOTS):
                    y, p = divmod(t, LOTS_B)
                    if turn.has_main:
                        blocks(turn, t)
                    if (y == 0 and turn.has_rest) or (y == 1 and turn.has_main):
                        post(p, 1 - y, turn.at(2, y))
                    if turn.has_main and (y == 0 or turn.pre_next):
                        pre(p, 1 - y, turn.at(2, y + 2))
                    if turn.has_rest:
                        layer1(t, turn)
                        layer2(t, turn)
                        layer3(t, turn)

            run_turns(act, body)

        @block.tensor
        def _(pe):
            def mm(dst, lhsT, rhs, start=True, stop=True):
                return pe.matmul(dst, lhsT, rhs, start=start, stop=stop)

            pe.wait_ge(gp_const, 2)
            pe.wait_ge(loaded, 16 * LOADS_COUNT)
            for j in range(NB):
                for i in range(NB):
                    last = pe.transpose(R0[:, j * N + i * P:j * N + (i + 1) * P], A[:, i, j * P:(j + 1) * P], ident[:])
            last.then_inc(pe_const, 1)
            for n, w in enumerate((raw2[:, 0], raw2[:, 1], rawu[:, 0], rawu[:, 1])):
                pe.transpose(R1[:, n * P:(n + 1) * P], w, ident[:])
            for n in range(3):
                for half in range(2):
                    last = mm(R2[:, n * P:(n + 1) * P], raw3[:, n, half * P:(half + 1) * P], ident[:], half == 0, half == 1)
            last.then_inc(pe_const, 1)
            pe.wait_ge(dve_const, DVE_CONST_TURNED)
            mm(PB[:, 0:P], qT, kT)
            for j in range(2):
                for c in range(EC):
                    mm(PC[:, j:j + 1], A[:, c, j * P:(j + 1) * P], a_lin[:, c:c + 1], c == 0, c == EC - 1)
            for c in range(EC):
                last = mm(PC[:, 2:3], a_lin_wide[:, c], b0_col[:, c:c + 1], c == 0, c == EC - 1)
            last.then_inc(pe_const, 1)
            pe.wait_ge(dve_const, DVE_CONST_ALL)

            def lot(turn, t):
                y, p = divmod(t, LOTS_B)
                row, c = divmod(p, EC)
                place, rnd = t % RING, t // RING
                if p == 0:
                    need(pe, score_ready, turn.at(2, y - 1))
                    pe.wait_ge(h0T_ready, turn.at(2, y + 1))
                    pe.matmul(S[y][:].rearrange("p (r j) -> p r j", r=NB), w2_lin_wide[:],
                              H0T[:, y].unsqueeze(1).to_broadcast([P, NB, N]), start=True, stop=False,
                              skip_group_check=True)
                pe.wait_ge(by_dve[place], turn.at(ROUNDS, rnd + 1))
                pe.wait_ge(by_act[place], turn.at(ROUNDS, rnd + 1))
                for g in range(GROUPS):
                    last = pe.matmul(S[y][g * ROWS:(g + 1) * ROWS, :], a_window[:, c, ROWS - 1 - row:2 * ROWS - 1 - row],
                                     ring[:, place, g], start=False, stop=p == LOTS_B - 1, skip_group_check=True)
                last.then_inc(freed[place], 1)

            def pre(p, y, value):
                if p == PRE["transpose"]:
                    pe.wait_ge(h0_ready, value)
                    for r in range(NB):
                        last = pe.transpose(PA[:, r * P:(r + 1) * P], H0[:, y, r], ident[:])
                    last.then_inc(h0T_psum, 1)
                if p == PRE["project"]:
                    pe.wait_ge(h0T_ready, value)
                    for r in range(NB):
                        mm(PA[:, N + r:N + r + 1], H0T[:, y, r * P:(r + 1) * P], w_lin[:, 0:1])
                    for j, bank_ in enumerate((PB, PC)):
                        for c in range(EC):
                            last = mm(bank_[:, c * N:(c + 1) * N], AT[:, j, c * P:(c + 1) * P], H0T[:, y])
                    last.then_inc(uv_psum, 1)

            def post(p, y, value):
                if p == POST["transpose"]:
                    pe.wait_ge(prob_ready, value)
                    for j in range(NB):
                        for i in range(NB):
                            last = pe.transpose(PB[:, j * N + i * P:j * N + (i + 1) * P], prob[:, i, j * P:(j + 1) * P], ident[:])
                    last.then_inc(probT_psum, 1)
                if p == POST["aggregate"]:
                    pe.wait_ge(probT_ready, value)
                    for i in range(NB):
                        for j in range(NB):
                            last = mm(PC[:, i * P:(i + 1) * P], probT[:, j, i * P:(i + 1) * P], H0[:, y, j], j == 0, j == NB - 1)
                    last.then_inc(attn_psum, 1)

            def turn_blocks(n, bank_, turn):
                for r in range(4):
                    last = pe.transpose(bank_[:, r * P:(r + 1) * P], h3[:, r] if n == 2 else normed[:, n, r], ident[:])
                last.then_inc(hT_psum[n], 1)

            def layer1(t, turn):
                pair = turn.at(1, 0)
                if t == LN1["transpose"]:
                    pe.wait_ge(ln_normed[0], pair)
                    turn_blocks(0, R0, turn)
                if t == L1["project"]:
                    pe.wait_ge(hT_ready[0], pair)
                    mm(R1[:], Wi[:], h1T[:]).then_inc(xh_psum, 1)
                if t == L1["edge_terms"]:
                    pe.wait_ge(xhT_ready, pair)
                    mm(R0[:], We_tgt_wide[:], xhT[:])
                    for n in range(4):
                        mm(R1[:, n:n + 1], xhT[:, n * P:(n + 1) * P], We[:, 0:1])
                    for n in range(4):
                        last = pe.transpose(R2[:, n * P:(n + 1) * P], xhT[:, n * P:(n + 1) * P], ident[:])
                    last.then_inc(edge_psum, 1)
                if t == L1["aggregate"]:
                    pe.wait_ge(xh_ready, pair)
                    pe.wait_ge(edge_ready, pair)
                    for y in range(2):
                        for r in range(NB):
                            mm(R2[:, y * N:(y + 1) * N], xh[:, NB * y + r], edge[:, y, r], r == 0, r == NB - 1)
                    for y in range(2):
                        for r in range(NB):
                            last = mm(R0[:, y * N:(y + 1) * N], ones[:], edge[:, y, r], r == 0, r == NB - 1)
                    last.then_inc(agg1_psum, 1)
                if t == L1["receive"]:
                    pe.wait_ge(aggT_ready, pair)
                    mm(R1[:], Wn[:, 0], aggT[:], True, False)
                    pe.wait_ge(selfT_ready, pair)
                    mm(R1[:], Wn[:, 1], selfT[:], False, True).then_inc(recv_psum, 1)
                if t == L1["out"]:
                    pe.wait_ge(recvT_ready, pair)
                    for n in range(4):
                        mm(R0[:, n * P:(n + 1) * P], recvT[:, n * P:(n + 1) * P], Wm[:, 0], True, False)
                        last = mm(R0[:, n * P:(n + 1) * P], xhT[:, n * P:(n + 1) * P], Wm[:, 1], False, True)
                    last.then_inc(out1_psum, 1)

            def layer2(t, turn):
                pair = turn.at(1, 0)
                if t == LN2["transpose"]:
                    pe.wait_ge(ln_normed[1], pair)
                    turn_blocks(1, R1, turn)
                if t == L2["project"]:
                    pe.wait_ge(hT_ready[1], pair)
                    mm(R2[:], G[:], h2T[:])
                    for n in range(4):
                        last = mm(R0[:, n * P:(n + 1) * P], h2T[:, n * P:(n + 1) * P], Wv[:])
                    last.then_inc(y_psum, 1)
                if t == L2["scores"]:
                    pe.wait_ge(yT_ready, pair)
                    for y, bank_ in enumerate((R1, R2)):
                        for r in range(NB):
                            n = NB * y + r
                            last = mm(bank_[:, r * N:(r + 1) * N], h2T[:, n * P:(n + 1) * P], YT[:, y * N:(y + 1) * N])
                    last.then_inc(logit_psum, 1)
                if t == L2["aggregate"]:
                    pe.wait_ge(weight2_ready, pair)
                    pe.wait_ge(hv_ready, pair)
                    for y, bank_ in enumerate((R0, R1)):
                        for i in range(NB):
                            for r in range(NB):
                                last = mm(bank_[:, i * (P + 1):(i + 1) * (P + 1)], weight2[:, y, r, i * P:(i + 1) * P],
                                          HV[:, NB * y + r], r == 0, r == NB - 1)
                    last.then_inc(agg2_psum, 1)

            def layer3(t, turn):
                pair = turn.at(1, 0)
                if t == LN3["transpose"]:
                    pe.wait_ge(h3_ready, pair)
                    turn_blocks(2, R2, turn)
                s, p = divmod(t - L3_AT, L3_PERIOD)
                if not 0 <= s < STEPS:
                    return
                step = turn.at(STEPS, s + 1 - STEPS)
                if p == L3["message"]:
                    if s == 0:
                        pe.wait_ge(hT_ready[2], pair)
                    else:
                        pe.wait_ge(state_back, turn.at(STEPS - 1, s + 1 - STEPS))
                    for y in range(2):
                        for r in range(NB):
                            last = mm(R0[:, y * N:(y + 1) * N], h3[:, NB * y + r], AT[:, r], r == 0, r == NB - 1)
                    last.then_inc(m_psum, 1)
                if p == L3["gates"]:
                    pe.wait_ge(mT_ready, step)
                    for n, bank_ in ((1, R2), (0, R1)):
                        mm(bank_[:], W345[:, n], mT[:], True, False)
                        last = mm(bank_[:], u3T, h3T[:], False, True)
                    last.then_inc(gates_psum, 1)
                if p == L3["candidate"]:
                    mm(R0[:], W345[:, 2], mT[:], True, False)
                    pe.wait_ge(rh_ready, step)
                    mm(R0[:], u5T_half, rh[:], False, True).then_inc(cand_psum, 1)
                if p == L3["transpose"]:
                    pe.wait_ge(state_ready, step)
                    pe.wait_ge(tz_ready, step)
                    for n in range(4):
                        last = pe.transpose(R1[:, n * P:(n + 1) * P], h3T[:, n * P:(n + 1) * P], ident[:])
                    last.then_inc(state_psum, 1)

            for p in sorted(PRE.values()):
                pre(p, 0, 1)

            def body(turn):
                for t in range(LOTS):
                    if turn.has_main:
                        lot(turn, t)
                    t += LEAD
                    if t >= LOTS:
                        continue
                    y, p = divmod(t, LOTS_B)
                    if (y == 0 and turn.has_rest) or (y == 1 and turn.has_main):
                        post(p, 1 - y, turn.at(2, y))
                    if turn.has_main and (y == 0 or turn.pre_next):
                        pre(p, 1 - y, turn.at(2, y + 2))
                    if turn.has_rest:
                        layer1(t, turn)
                        layer2(t, turn)
                        layer3(t, turn)

            run_turns(pe, body)


_INS = ["x", "adj", "L0_gnn_b_lin", "L0_gnn_a", "L1_gnn_Wi", "L1_gnn_bi", "L1_gnn_We", "L1_gnn_be", "L1_gnn_Wn",
        "L1_gnn_bn", "L1_gnn_Wm", "L1_gnn_bm", "L2_gnn_q", "L2_gnn_k", "L2_gnn_v", "L3_gnn_w3_w", "L3_gnn_w3_b",
        "L3_gnn_u3_w", "L3_gnn_u3_b", "L3_gnn_w4_w", "L3_gnn_w4_b", "L3_gnn_w5_w", "L3_gnn_w5_b", "L3_gnn_u5_w",
        "L3_gnn_u5_b"]


def kernel(**inputs):
    import numpy as np
    import concourse.bacc as bacc
    from concourse.bass_utils import run_bass_kernel_spmd

    nc = bacc.Bacc("TRN2", target_bir_lowering=False, num_devices=1)
    arrays, args = {}, []
    for name in _INS:
        a = np.ascontiguousarray(inputs[name])
        arrays[f"in_{name}"] = a
        args.append(nc.dram_tensor(f"in_{name}", a.shape, mybir.dt.from_np(a.dtype), kind="ExternalInput").ap())
    out = nc.dram_tensor("out", inputs["x"].shape, F32, kind="ExternalOutput").ap()
    gnn_stack(nc, *args, out)
    results = run_bass_kernel_spmd(nc, [arrays], core_ids=[0])
    return results.results[0]["out"]
```

```python
from contextlib import ExitStack

import concourse.bass as bass
from concourse import mybir

F32 = mybir.dt.float32
ALU = mybir.AluOpType
ACT = mybir.ActivationFunctionType
AXIS = mybir.AxisListType

P = 128
N = 256
NB = N // P
E = 256
EC = E // P
NEG_SLOPE0 = 0.2
MASK_ALPHA1 = 0.005
LN_EPS = 1e-5
STEPS = 5
LOGIT_BOUND2 = 8.0

GROUPS = 4
ROWS = P // GROUPS
LOTS_B = EC * ROWS
LOTS = 2 * LOTS_B
BLOCKS = GROUPS * NB
RING = 8
ROUNDS = LOTS // RING

LEAD = 4
POST = dict(score=5, exp=6, transpose=10, copy=11, aggregate=12, tanh=14, residual=15)
PRE = dict(stats=40, norm=43, transpose=46, copy=48, project=56, evacuate=61)
LN1 = dict(stats=17, norm=20, transpose=22, copy=24)
L1 = dict(project=26, exp=28, elu=29, edge_terms=31, edge_copy=33, tanh=34, mask=36, aggregate=39, agg_copy=42,
          receive=44, recv_exp=46, recv_elu=47, out=50, residual=53)
LN2 = dict(stats=56, norm=59, transpose=68, copy=70)
L2 = dict(project=73, copy=77, scores=80, tanh=84, exp=86, mask=89, aggregate=94, residual=100)
LN3 = dict(stats=2, norm=5, transpose=8, copy=10)
L3_AT, L3_PERIOD = 12, 22
L3 = dict(message=0, copy=2, gates=4, reset=7, update=8, candidate=10, z_gate=12, tanh=13, state=15, transpose=18, back=20)

SRC_COLS = slice(2 * N - 4, 2 * N)
LOADS_COUNT = 24
DVE_CONST_TURNED, DVE_CONST_ALL = 10, 13

VECTOR_BLOCK, SCALAR_BLOCK = 2.63, 3.57


def stage_costs():
    vector, scalar = [0.0] * LOTS, [0.0] * LOTS

    def put(costs, table, at, **stages):
        for name, cost in stages.items():
            costs[at + table[name]] += cost

    for half in (0, LOTS_B):
        put(vector, POST, half, score=7, transpose=1.5, residual=3.4)
        put(scalar, POST, half, exp=10, copy=4.8, tanh=5)
        put(vector, PRE, half, stats=5.5, evacuate=8.5)
        put(scalar, PRE, half, norm=5, copy=2.6, evacuate=4.8)
    for ln in (LN1, LN2, LN3):
        put(vector, ln, 0, stats=11, norm=10 if ln is not LN3 else 0)
        put(scalar, ln, 0, norm=10 if ln is LN3 else 0, copy=4.8)
    put(vector, L1, 0, elu=10, edge_copy=1.3, mask=12, agg_copy=6, recv_elu=10, residual=6)
    put(scalar, L1, 0, exp=5.7, edge_copy=4.8, tanh=14.2, agg_copy=4.8, recv_exp=5.7)
    put(vector, L2, 0, copy=6, mask=11.4, residual=11.8)
    put(scalar, L2, 0, copy=4.8, tanh=9.6, exp=9.5)
    for s in range(STEPS):
        put(vector, L3, L3_AT + s * L3_PERIOD, update=6, state=18)
        put(scalar, L3, L3_AT + s * L3_PERIOD, copy=4.8, reset=5.7, z_gate=5.7, tanh=5.7, back=4.8 if s < STEPS - 1 else 0)
    return vector, scalar


def share_blocks():
    vector, scalar = stage_costs()
    shares, v, s = [], 0.0, 0.0
    for t in range(LOTS):
        n = min(range(1, BLOCKS), key=lambda n: max(v + (BLOCKS - n) * VECTOR_BLOCK, s + n * SCALAR_BLOCK))
        shares.append(n)
        v += (BLOCKS - n) * VECTOR_BLOCK + vector[t]
        s += n * SCALAR_BLOCK + scalar[t]
    return shares


ACT_BLOCKS = share_blocks()


def gnn_stack(nc, x, adj, L0_b, L0_a, L1_Wi, L1_bi, L1_We, L1_be, L1_Wn, L1_bn, L1_Wm, L1_bm, L2_q, L2_k, L2_v,
              L3_w3_w, L3_w3_b, L3_u3_w, L3_u3_b, L3_w4_w, L3_w4_b, L3_w5_w, L3_w5_b, L3_u5_w, L3_u5_b, out):
    BATCHES = x.shape[0]
    PAIRS = BATCHES // 2
    x_rows = x.rearrange("b (r p) d -> b p r d", p=P)
    out_rows = out.rearrange("b (r p) d -> b p r d", p=P)

    class Turn:

        def __init__(self, m=None, it=None):
            self.m, self.it = m, it
            self.has_main = it is not None or m < PAIRS
            self.has_post = [it is not None or 1 <= m <= PAIRS, self.has_main]
            self.has_l12 = it is not None or 1 <= m <= PAIRS
            self.has_l3 = it is not None or m >= 2
            self.pre_next = it is not None or m < PAIRS - 1

        def at(self, per_turn, more):
            if self.it is None:
                return per_turn * self.m + more
            return self.it * per_turn + (2 * per_turn + more)

    def need(eng, sem, value):
        if isinstance(value, int) and value <= 0:
            return
        eng.wait_ge(sem, value)

    def run_turns(eng, body):
        for m in range(2):
            body(Turn(m=m))
        with eng.Fori(0, PAIRS - 3) as it:
            body(Turn(it=it))
        for m in range(PAIRS - 1, PAIRS + 2):
            body(Turn(m=m))

    with ExitStack() as ctx:
        def sb(name, shape):
            return ctx.enter_context(nc.sbuf_tensor(name, shape, F32))

        def bank(name):
            return ctx.enter_context(nc.psum_tensor(name, [P, 512], F32))

        def sem(name):
            return ctx.enter_context(nc.semaphore(name))

        ident = sb("ident", [P, P])
        ones = sb("ones", [P, P])
        eps = sb("eps", [P, 4])
        minus_one = sb("minus_one", [P, 4])
        minus_half = sb("minus_half", [P, 4])
        A = sb("A", [P, NB, N])
        AT = sb("AT", [P, NB, N])
        a_col = sb("a_col", [P, EC])
        a_lin = sb("a_lin", [P, EC])
        a_lin_wide = sb("a_lin_wide", [P, EC, P])
        a_window = sb("a_window", [P, EC, 2 * ROWS - 1])
        b0_col = sb("b0_col", [P, EC])
        w_lin = sb("w_lin", [P, 3])
        w2_lin_wide = sb("w2_lin_wide", [P, P])
        A_bias = sb("A_bias", [P, NB, N])
        maskT = sb("maskT", [P, NB, N])
        maskT_tmp = sb("maskT_tmp", [P, NB, N])
        Wi = sb("Wi", [P, P])
        We = sb("We", [P, 2])
        be = sb("be", [P, 1])
        We_tgt_wide = sb("We_tgt_wide", [P, P])
        Wn = sb("Wn", [P, 2, P])
        Wm = sb("Wm", [P, 2, P])
        bm_half = sb("bm_half", [1, P])
        cols = sb("cols", [P, 7])
        bias3 = sb("bias3", [P, 3])
        raw2 = sb("raw2", [P, 2, P])
        Wv = sb("Wv", [P, P])
        raw3 = sb("raw3", [P, 3, 2 * P])
        rawu = sb("rawu", [P, 2, P])
        turned = sb("turned", [P, 4, P])
        G = sb("G", [P, P])
        W345 = sb("W345", [P, 3, P])
        qT, kT, u3T, u5T_half = (turned[:, n, :] for n in range(4))

        X0 = sb("X0", [P, 2, NB, P])
        H0 = sb("H0", [P, 2, NB, P])
        H0T = sb("H0T", [P, 2, N])
        U = sb("U", [P, 2, EC, N])
        V = sb("V", [P, 2, EC, N])
        lin_i = sb("lin_i", [P, 2, NB])
        ring = sb("ring", [P, RING, GROUPS, NB * N])
        st0 = sb("st0", [P, NB, 6])
        mv0 = sb("mv0", [P, NB, 2])
        var0 = sb("var0", [P, NB])
        rstd0 = sb("rstd0", [P, NB])
        minus_mean0 = sb("minus_mean0", [P, NB])
        shift0 = sb("shift0", [P, NB])
        prob = sb("prob", [P, NB, N])
        probT = sb("probT", [P, NB, N])
        neg_max = sb("neg_max", [P, NB])
        exp_bias = sb("exp_bias", [P, NB])
        row_sum = sb("row_sum", [P, NB])
        inv_sum = sb("inv_sum", [P, NB])
        half_inv = sb("half_inv", [P, NB])
        tanh0 = sb("tanh0", [P, NB, P])

        X1 = sb("X1", [P, 4, P])
        X2 = sb("X2", [P, 4, P])
        X3 = sb("X3", [P, 4, P])
        X3_held = sb("X3_held", [P, 4, P])
        OUT = sb("OUT", [P, 4, P])
        st = sb("st", [P, 3, 4, 6])
        wait_carrier = sb("wait_carrier", [P, 1])
        mv = sb("mv", [P, 3, 4, 2])
        var = sb("var", [P, 3, 4])
        rstd = sb("rstd", [P, 3, 4])
        normed = sb("normed", [P, 2, 4, P])
        minus_mean3 = sb("minus_mean3", [P, 4])
        shift3 = sb("shift3", [P, 4])
        h1T = sb("h1T", [P, 2 * N])
        exp1 = sb("exp1", [P, 2 * N])
        xhT = sb("xhT", [P, 2 * N])
        xh = sb("xh", [P, 4, P])
        src_bias = sb("src_bias", [P, 4])
        edge = sb("edge", [P, 2, NB, N])
        aggT = sb("aggT", [P, 2 * N])
        selfT = sb("selfT", [P, 2 * N])
        exp1r = sb("exp1r", [P, 2 * N])
        recvT = sb("recvT", [P, 2 * N])
        h2T = sb("h2T", [P, 2 * N])
        YT = sb("YT", [P, 2 * N])
        HV = sb("HV", [P, 4, P + 1])
        logit2 = sb("logit2", [P, 2, NB, N])
        weight2 = sb("weight2", [P, 2, NB, N])
        inv2 = sb("inv2", [P, 4])
        h3T = sb("h3T", [P, 2 * N])
        h3 = sb("h3", [P, 4, P])
        mT = sb("mT", [P, 2 * N])
        tr = sb("tr", [P, 2 * N])
        tz = sb("tz", [P, 2 * N])
        rh = sb("rh", [P, 2 * N])
        cand = sb("cand", [P, 2 * N])
        diff = sb("diff", [P, 2 * N])
        gated = sb("gated", [P, 2 * N])

        S = [bank("S0"), bank("S1")]
        V_bank = [bank("V0"), bank("V1")]
        PA, PB = bank("PA"), bank("PB")
        R0, R1 = bank("R0"), bank("R1")

        loaded = sem("loaded")
        gp_const, dve_const, pe_const = sem("gp_const"), sem("dve_const"), sem("pe_const")
        by_dve = [sem(f"by_dve{n}") for n in range(RING)]
        by_act = [sem(f"by_act{n}") for n in range(RING)]
        freed = [sem(f"freed{n}") for n in range(RING)]
        x_loaded, pre_stats, pre_mv, pre_eps, pre_rstd = (sem(n) for n in "x_loaded pre_stats pre_mv pre_eps pre_rstd".split())
        pre_shift, h0_ready, h0T_psum, h0T_ready = (sem(n) for n in "pre_shift h0_ready h0T_psum h0T_ready".split())
        uv_psum, u_ready, v_ready = (sem(n) for n in "uv_psum u_ready v_ready".split())
        max_ready, exp_bias_ready, prob_ready = (sem(n) for n in "max_ready exp_bias_ready prob_ready".split())
        probT_psum, probT_ready, inv_ready, half_inv_ready = (sem(n) for n in "probT_psum probT_ready inv_ready half_inv_ready".split())
        attn_psum, tanh0_ready, x1_ready = (sem(n) for n in "attn_psum tanh0_ready x1_ready".split())
        ln_stats = [sem(f"ln{n}_stats") for n in (1, 2, 3)]
        ln_mv = [sem(f"ln{n}_mv") for n in (1, 2, 3)]
        ln_eps = [sem(f"ln{n}_eps") for n in (1, 2, 3)]
        ln_rstd = [sem(f"ln{n}_rstd") for n in (1, 2, 3)]
        ln_normed = [sem(f"ln{n}_normed") for n in (1, 2)]
        ln3_shift = sem("ln3_shift")
        hT_psum = [sem(f"h{n}T_psum") for n in (1, 2, 3)]
        hT_ready = [sem(f"h{n}T_ready") for n in (1, 2, 3)]
        xh_psum, xh_exp, xh_min, xhT_ready = (sem(n) for n in "xh_psum xh_exp xh_min xhT_ready".split())
        edge_psum, src_ready, xh_ready, edge_tanh, edge_ready = (sem(n) for n in "edge_psum src_ready xh_ready edge_tanh edge_ready".split())
        agg1_psum, aggT_ready, selfT_ready = (sem(n) for n in "agg1_psum aggT_ready selfT_ready".split())
        recv_psum, recv_exp, recv_min, recvT_ready = (sem(n) for n in "recv_psum recv_exp recv_min recvT_ready".split())
        out1_psum, x2_ready = sem("out1_psum"), sem("x2_ready")
        y_psum, yT_ready, hv_ready, logit_psum, tanh2_ready = (sem(n) for n in "y_psum yT_ready hv_ready logit_psum tanh2_ready".split())
        exp2_ready, weight2_ready, agg2_psum, inv2_ready, x3_ready = (sem(n) for n in "exp2_ready weight2_ready agg2_psum inv2_ready x3_ready".split())
        x3_held, h3_ready = sem("x3_held"), sem("h3_ready")
        m_psum, mT_ready, r_psum, tr_ready, rh_ready, z_psum, tz_ready = (sem(n) for n in "m_psum mT_ready r_psum tr_ready rh_ready z_psum tz_ready".split())
        cand_psum, cand_ready, diff_ready, gated_ready = (sem(n) for n in "cand_psum cand_ready diff_ready gated_ready".split())
        state_ready, state_psum, state_back = (sem(n) for n in "state_ready state_psum state_back".split())
        out_ready, out_stored = sem("out_ready"), sem("out_stored")

        block = ctx.enter_context(nc.Block())

        @block.sync
        def _(sp):
            def load(dst, src):
                sp.dma_start(dst, src, allow_slow_non_contiguous=True).then_inc(loaded, 16)
                count[0] += 1

            count = [0]
            sp.sem_inc(out_stored, 16)
            sp.dma_start(X0[:, 0], x_rows[0]).then_inc(x_loaded, 16)
            load(A[:], adj.rearrange("(r p) j -> p r j", p=P))
            load(a_col[:], L0_a.rearrange("(c p) -> p c", p=P))
            load(b0_col[:], L0_b.rearrange("(c p) -> p c", p=P))
            load(Wi[:], L1_Wi)
            load(We[:], L1_We.rearrange("(c p) o -> p (c o)", p=P))
            load(be[:], L1_be.partition_broadcast(P))
            load(Wn[:], L1_Wn.rearrange("(c p) o -> p c o", p=P))
            load(Wm[:], L1_Wm.rearrange("(c p) o -> p c o", p=P))
            load(bm_half[:], L1_bm.rearrange("(o d) -> o d", o=1))
            for n, b in enumerate((L1_bi, L1_bn, L3_w3_b, L3_w4_b, L3_w5_b, L3_u3_b, L3_u5_b)):
                load(cols[:, n:n + 1], b.rearrange("(p o) -> p o", o=1))
            load(raw2[:, 0], L2_q)
            load(raw2[:, 1], L2_k)
            load(Wv[:], L2_v)
            for n, w in enumerate((L3_w3_w, L3_w4_w, L3_w5_w)):
                load(raw3[:, n], w)
            load(rawu[:, 0], L3_u3_w)
            load(rawu[:, 1], L3_u5_w)
            assert count[0] == LOADS_COUNT, count

            def body(turn):
                for y in range(2):
                    if turn.has_main and (y == 0 or turn.pre_next):
                        need(sp, x1_ready, turn.at(2, y))
                        b = turn.at(2, y + 1)
                        sp.dma_start(X0[:, 1 - y], x_rows[b] if isinstance(b, int) else x_rows[bass.ds(b, 1)].rearrange("o p r d -> (o p) r d")).then_inc(x_loaded, 16)
                if turn.has_l3:
                    sp.wait_ge(out_ready, turn.at(1, -1))
                    for y in range(2):
                        b = turn.at(2, y - 4)
                        dst = out_rows[b] if isinstance(b, int) else out_rows[bass.ds(b, 1)].rearrange("o p r d -> (o p) r d")
                        sp.dma_start(dst, OUT[:, NB * y:NB * y + NB]).then_inc(out_stored, 16)
                if turn.has_l12:
                    sp.wait_ge(x3_ready, turn.at(1, 0))
                    sp.dma_start(X3_held[:], X3[:]).then_inc(x3_held, 16)

            run_turns(sp, body)
            sp.wait_ge(out_stored, 16 * (BATCHES + 1))

        @block.gpsimd
        def _(gp):
            gp.memset(ident[:], 0.0).then_inc(gp_const, 1)
            gp.wait_ge(gp_const, 1)
            gp.affine_select(out=ident[:], in_=ident[:], compare_op=ALU.not_equal, fill=1.0, base=0,
                             pattern=[[-1, P]], channel_multiplier=1).then_inc(gp_const, 1)
            gp.wait_ge(dve_const, 1)

            def norm_factors(mean, var_, with_shift, rstd_, width, sem_in, sem_eps, sem_rstd, value):
                gp.wait_ge(sem_in, value)
                if with_shift:
                    gp.tensor_tensor(with_shift[0], mean, minus_one[:, 0:width], ALU.mult)
                gp.tensor_tensor(var_[1], var_[0], eps[:, 0:width], ALU.add).then_inc(sem_eps, 1)
                gp.wait_ge(sem_eps, value)
                gp.tensor_tensor(rstd_, var_[1], minus_half[:, 0:width], ALU.pow).then_inc(sem_rstd, 1)
                if with_shift:
                    gp.wait_ge(sem_rstd, value)
                    gp.tensor_tensor(with_shift[1], with_shift[0], rstd_, ALU.mult).then_inc(with_shift[2], 1)

            def pre(value):
                norm_factors(mv0[:, :, 0], (mv0[:, :, 1], var0[:]), (minus_mean0[:], shift0[:], pre_shift), rstd0[:], NB,
                             pre_mv, pre_eps, pre_rstd, value)

            def norm(n, turn):
                norm_factors(mv[:, n, :, 0], (mv[:, n, :, 1], var[:, n]),
                             (minus_mean3[:], shift3[:], ln3_shift) if n == 2 else None, rstd[:, n], 4,
                             ln_mv[n], ln_eps[n], ln_rstd[n], turn.at(1, -(n // 2)))

            pre(1)

            def body(turn):
                for t in range(LOTS):
                    y, p = divmod(t, LOTS_B)
                    if p == PRE["stats"] and turn.has_main and (y == 0 or turn.pre_next):
                        pre(turn.at(2, y + 2))
                    for n, (ln, runs) in enumerate(((LN1, turn.has_l12), (LN2, turn.has_l12), (LN3, turn.has_l3))):
                        if t == ln["stats"] and runs:
                            norm(n, turn)

            run_turns(gp, body)

        @block.vector
        def _(dve):
            chain = [1]

            def constant(ins):
                chain[0] += 1
                ins.then_inc(dve_const, 1)
                dve.wait_ge(dve_const, chain[0])

            dve.memset(eps[:], LN_EPS)
            dve.memset(minus_one[:], -1.0)
            dve.memset(minus_half[:], -0.5).then_inc(dve_const, 1)
            dve.memset(ones[:], 1.0)
            dve.memset(HV[:, :, P:P + 1], 1.0)
            constant(dve.memset(a_window[:], 0.0))
            dve.wait_ge(loaded, 16 * LOADS_COUNT)
            dve.tensor_scalar(a_window[:, :, ROWS - 1:ROWS], a_col[:].unsqueeze(2), 1.0 - NEG_SLOPE0, None, ALU.mult)
            constant(dve.tensor_scalar(a_lin[:], a_col[:], NEG_SLOPE0, None, ALU.mult))
            dve.tensor_copy(We_tgt_wide[:], We[:, 1:2].to_broadcast([P, P]))
            dve.tensor_tensor(bias3[:, 0:2], cols[:, 2:4], cols[:, 5:6].to_broadcast([P, 2]), ALU.add)
            dve.tensor_tensor(bias3[:, 2:3], cols[:, 4:5], cols[:, 6:7], ALU.add)
            dve.tensor_scalar(bm_half[:], bm_half[:], 0.5, None, ALU.add)
            constant(dve.tensor_copy(a_lin_wide[:], a_lin[:].unsqueeze(2).to_broadcast([P, EC, P])))
            constant(dve.tensor_scalar(bias3[:, 0:2], bias3[:, 0:2], 0.5, None, ALU.mult))
            dve.wait_ge(pe_const, 1)
            constant(dve.tensor_copy(AT[:], R0[:].rearrange("p (r i) -> p r i", r=NB)))
            constant(dve.tensor_scalar(maskT_tmp[:], AT[:], 0.0, -0.5 * MASK_ALPHA1, ALU.not_equal, ALU.mult))
            constant(dve.tensor_scalar(maskT_tmp[:], maskT_tmp[:], 0.5 * MASK_ALPHA1, None, ALU.add))
            constant(dve.scalar_tensor_tensor(maskT[:], AT[:], 0.5, maskT_tmp[:], ALU.mult, ALU.add))
            dve.wait_ge(pe_const, 2)
            dve.tensor_copy(turned[:, 0:3], R1[:, 0:3 * P].rearrange("p (n k) -> p n k", n=3))
            dve.tensor_scalar(turned[:, 3], R1[:, 3 * P:4 * P], 0.5, None, ALU.mult)
            constant(dve.tensor_copy(W345[:], PB[:, 0:3 * P].rearrange("p (n k) -> p n k", n=3)))
            at_const_ready = chain[0]
            constant(dve.tensor_tensor(W345[:, 0], W345[:, 0], W345[:, 1], ALU.subtract))
            dve.wait_ge(pe_const, 3)
            dve.tensor_copy(G[:], R0[:, 0:P])
            constant(dve.tensor_copy(w_lin[:], R1[:, 0:3]))
            dve.tensor_copy(w2_lin_wide[:], w_lin[:, 1:2].to_broadcast([P, P]))
            constant(dve.tensor_scalar(A_bias[:], A[:], w_lin[:, 2:3], None, ALU.add))
            assert (at_const_ready, chain[0]) == (DVE_CONST_TURNED, DVE_CONST_ALL), (at_const_ready, chain[0])

            def blocks(turn, t):
                y, p = divmod(t, LOTS_B)
                row, c = divmod(p, EC)
                place, rnd = t % RING, t // RING
                need(dve, freed[place], turn.at(ROUNDS, rnd))
                if p == 0:
                    dve.wait_ge(u_ready, turn.at(2, y + 1))
                    dve.wait_ge(v_ready, turn.at(2, y + 1))
                for n in range(BLOCKS - ACT_BLOCKS[t]):
                    g, half = divmod(n, NB)
                    i = half * P + g * ROWS + row
                    last = dve.tensor_scalar(ring[:, place, g, half * N:(half + 1) * N], V[:, y, c],
                                             U[:, y, c, i:i + 1], 0.0, ALU.add, ALU.max)
                last.then_inc(by_dve[place], 1)

            def pre(p, y, value):
                if p == PRE["stats"]:
                    dve.wait_ge(x_loaded, value * 16)
                    for r in range(NB):
                        last = dve.bn_stats(st0[:, r], X0[:, y, r])
                    last.then_inc(pre_stats, 1)
                    dve.wait_ge(pre_stats, value)
                    dve.memset(wait_carrier[:], 0.0)
                    for r in range(NB):
                        last = dve.bn_aggr(mv0[:, r], st0[:, r])
                    last.then_inc(pre_mv, 1)
                if p == PRE["evacuate"]:
                    dve.wait_ge(uv_psum, value)
                    dve.tensor_copy(lin_i[:, y], PA[:, N:N + NB])
                    for c in range(EC):
                        last = dve.tensor_scalar(U[:, y, c], PB[:, c * N:(c + 1) * N], b0_col[:, c:c + 1], None, ALU.add)
                    last.then_inc(u_ready, 1)

            def post(p, y, value, lots_done):
                if p == POST["score"]:
                    dve.wait_ge(freed[RING - 1], lots_done)
                    dve.tensor_reduce(neg_max[:], S[y][:].rearrange("p (r j) -> p r j", r=NB), AXIS.X, ALU.max,
                                      negate=True).then_inc(max_ready, 1)
                    dve.wait_ge(max_ready, value)
                    for r in range(NB):
                        last = dve.scalar_tensor_tensor(exp_bias[:, r:r + 1], neg_max[:, r:r + 1], lin_i[:, y, r:r + 1],
                                                        lin_i[:, y, r:r + 1], ALU.subtract, ALU.add)
                    last.then_inc(exp_bias_ready, 1)
                if p == POST["transpose"]:
                    dve.wait_ge(prob_ready, value)
                    dve.reciprocal(inv_sum[:], row_sum[:]).then_inc(inv_ready, 1)
                    dve.wait_ge(inv_ready, value)
                    dve.tensor_scalar(half_inv[:], inv_sum[:], 0.5, None, ALU.mult).then_inc(half_inv_ready, 1)
                if p == POST["residual"]:
                    dve.wait_ge(tanh0_ready, value)
                    dve.scalar_tensor_tensor(X1[:, NB * y:NB * y + NB], tanh0[:], 0.5, X0[:, y], ALU.mult,
                                             ALU.add).then_inc(x1_ready, 1)

            def norm(t, ln, n, src, pair):
                if t == ln["stats"]:
                    for r in range(4):
                        last = dve.bn_stats(st[:, n, r], src[:, r])
                    last.then_inc(ln_stats[n], 1)
                    dve.wait_ge(ln_stats[n], pair)
                    dve.memset(wait_carrier[:], 0.0)
                    for r in range(4):
                        last = dve.bn_aggr(mv[:, n, r], st[:, n, r])
                    last.then_inc(ln_mv[n], 1)
                if t == ln["norm"] and n < 2:
                    dve.wait_ge(ln_rstd[n], pair)
                    for r in range(4):
                        last = dve.tensor_scalar(normed[:, n, r], src[:, r], mv[:, n, r, 0:1], rstd[:, n, r:r + 1],
                                                 ALU.subtract, ALU.mult)
                    last.then_inc(ln_normed[n], 1)

            def elu(bank_, bias, exp_, dst, sem_exp, sem_min, sem_out, turn):
                dve.wait_ge(sem_exp, turn.at(1, 0))
                dve.tensor_scalar(exp_[:], exp_[:], 1.0, 1.0, ALU.min, ALU.subtract).then_inc(sem_min, 1)
                dve.wait_ge(sem_min, turn.at(1, 0))
                dve.scalar_tensor_tensor(dst[:], bank_[:], bias, exp_[:], ALU.add, ALU.max).then_inc(sem_out, 1)

            def layer1(t, turn):
                pair = turn.at(1, 0)
                if t == LN1["stats"]:
                    dve.wait_ge(x1_ready, turn.at(2, 0))
                norm(t, LN1, 0, X1, pair)
                if t == L1["elu"]:
                    elu(V_bank[1], cols[:, 0:1], exp1, xhT, xh_exp, xh_min, xhT_ready, turn)
                if t == L1["edge_copy"]:
                    dve.wait_ge(edge_psum, pair)
                    dve.tensor_scalar(src_bias[:], PA[:, SRC_COLS], be[:], 0.5, ALU.add, ALU.mult).then_inc(src_ready, 1)
                if t == L1["mask"]:
                    dve.wait_ge(edge_tanh, pair)
                    for y in range(2):
                        last = dve.scalar_tensor_tensor(edge[:, y], edge[:, y], 1.0, maskT[:], ALU.add, ALU.mult)
                    last.then_inc(edge_ready, 1)
                if t == L1["agg_copy"]:
                    dve.wait_ge(agg1_psum, pair)
                    dve.tensor_tensor(selfT[:], xhT[:], S[1][:], ALU.mult).then_inc(selfT_ready, 1)
                if t == L1["recv_elu"]:
                    elu(V_bank[1], cols[:, 1:2], exp1r, recvT, recv_exp, recv_min, recvT_ready, turn)
                if t == L1["residual"]:
                    dve.wait_ge(out1_psum, pair)
                    dve.tensor_tensor(X2[:], S[1][:].rearrange("p (r d) -> p r d", r=4), X1[:],
                                      ALU.add).then_inc(x2_ready, 1)

            def layer2(t, turn):
                pair = turn.at(1, 0)
                if t == LN2["stats"]:
                    dve.wait_ge(x2_ready, pair)
                norm(t, LN2, 1, X2, pair)
                if t == L2["copy"]:
                    dve.wait_ge(y_psum, pair)
                    dve.tensor_copy(HV[:, :, 0:P], V_bank[0][:].rearrange("p (r d) -> p r d", r=4)).then_inc(hv_ready, 1)
                if t == L2["mask"]:
                    dve.wait_ge(exp2_ready, pair)
                    dve.tensor_tensor(weight2[:], weight2[:], AT[:].unsqueeze(1).to_broadcast([P, 2, NB, N]),
                                      ALU.mult).then_inc(weight2_ready, 1)
                if t == L2["residual"]:
                    dve.wait_ge(agg2_psum, pair)
                    for y, bank_ in enumerate((S[0], V_bank[0])):
                        sums = bank_[:, 0:NB * (P + 1)].rearrange("p (r d) -> p r d", r=NB)
                        last = dve.reciprocal(inv2[:, NB * y:NB * y + NB], sums[:, :, P])
                    last.then_inc(inv2_ready, 1)
                    dve.wait_ge(inv2_ready, pair)
                    for n in range(4):
                        bank_, r = (S[0], V_bank[0])[n // NB], n % NB
                        last = dve.scalar_tensor_tensor(X3[:, n], bank_[:, r * (P + 1):r * (P + 1) + P], inv2[:, n:n + 1],
                                                        X2[:, n], ALU.mult, ALU.add)
                    last.then_inc(x3_ready, 1)

            def layer3(t, turn):
                pair = turn.at(1, -1)
                if t == LN3["stats"]:
                    dve.wait_ge(x3_held, turn.at(16, -16))
                norm(t, LN3, 2, X3_held, pair)
                s, p = divmod(t - L3_AT, L3_PERIOD)
                if not 0 <= s < STEPS:
                    return
                step = turn.at(STEPS, s + 1 - 2 * STEPS)
                if p == L3["update"]:
                    dve.wait_ge(tr_ready, step)
                    dve.scalar_tensor_tensor(rh[:], tr[:], 1.0, h3T[:], ALU.add, ALU.mult).then_inc(rh_ready, 1)
                if p == L3["state"]:
                    dve.wait_ge(cand_ready, step)
                    dve.tensor_tensor(diff[:], cand[:], h3T[:], ALU.subtract).then_inc(diff_ready, 1)
                    dve.wait_ge(diff_ready, step)
                    dve.wait_ge(tz_ready, step)
                    dve.scalar_tensor_tensor(gated[:], tz[:], 1.0, diff[:], ALU.add, ALU.mult).then_inc(gated_ready, 1)
                    dve.wait_ge(gated_ready, step)
                    dve.scalar_tensor_tensor(h3T[:], gated[:], 0.5, h3T[:], ALU.mult, ALU.add).then_inc(state_ready, 1)
                if p == L3["back"] and s == STEPS - 1:
                    dve.wait_ge(state_psum, step)
                    dve.wait_ge(out_stored, turn.at(32, -48))
                    dve.tensor_tensor(OUT[:], R1[:].rearrange("p (r d) -> p r d", r=4), X3_held[:], ALU.add).then_inc(out_ready, 1)

            for p in sorted(PRE.values()):
                pre(p, 0, 1)

            def body(turn):
                for t in range(LOTS):
                    y, p = divmod(t, LOTS_B)
                    if turn.has_main:
                        blocks(turn, t)
                    if turn.has_post[y]:
                        post(p, 1 - y, turn.at(2, y), turn.at(ROUNDS, y * ROUNDS // 2))
                    if turn.has_main and (y == 0 or turn.pre_next):
                        pre(p, 1 - y, turn.at(2, y + 2))
                    if turn.has_l12:
                        layer1(t, turn)
                        layer2(t, turn)
                    if turn.has_l3:
                        layer3(t, turn)

            run_turns(dve, body)

        @block.scalar
        def _(act):
            def blocks(turn, t):
                y, p = divmod(t, LOTS_B)
                row, c = divmod(p, EC)
                place, rnd = t % RING, t // RING
                need(act, freed[place], turn.at(ROUNDS, rnd))
                if p == 0:
                    act.wait_ge(u_ready, turn.at(2, y + 1))
                for n in range(BLOCKS - ACT_BLOCKS[t], BLOCKS):
                    g, half = divmod(n, NB)
                    i = half * P + g * ROWS + row
                    last = act.activation(ring[:, place, g, half * N:(half + 1) * N], V_bank[y][:, c * N:(c + 1) * N], ACT.Relu,
                                          bias=U[:, y, c, i:i + 1])
                last.then_inc(by_act[place], 1)

            def pre(p, y, value):
                if p == PRE["norm"]:
                    act.wait_ge(pre_shift, value)
                    for r in range(NB):
                        last = act.activation(H0[:, y, r], X0[:, y, r], ACT.Relu, bias=shift0[:, r:r + 1], scale=rstd0[:, r:r + 1])
                    last.then_inc(h0_ready, 1)
                if p == PRE["copy"]:
                    act.wait_ge(h0T_psum, value)
                    act.activation(H0T[:, y], PA[:, 0:N], ACT.Copy).then_inc(h0T_ready, 1)
                if p == PRE["evacuate"]:
                    act.wait_ge(uv_psum, value)
                    act.activation(V[:, y], V_bank[y][:].rearrange("p (c n) -> p c n", c=EC), ACT.Copy).then_inc(v_ready, 1)

            def post(p, y, value):
                if p == POST["exp"]:
                    act.wait_ge(exp_bias_ready, value)
                    for r in range(NB):
                        last = act.activation(prob[:, r], S[y][:, r * N:(r + 1) * N], ACT.Exp, bias=exp_bias[:, r:r + 1],
                                              accum_out=row_sum[:, r:r + 1])
                    last.then_inc(prob_ready, 1)
                if p == POST["copy"]:
                    act.wait_ge(probT_psum, value)
                    act.activation(probT[:], PB[:].rearrange("p (r i) -> p r i", r=NB), ACT.Copy).then_inc(probT_ready, 1)
                if p == POST["tanh"]:
                    act.wait_ge(attn_psum, value)
                    act.wait_ge(half_inv_ready, value)
                    for r in range(NB):
                        last = act.activation(tanh0[:, r], PA[:, r * P:(r + 1) * P], ACT.Tanh, scale=half_inv[:, r:r + 1])
                    last.then_inc(tanh0_ready, 1)

            def layer1(t, turn):
                pair = turn.at(1, 0)
                if t == LN1["copy"]:
                    act.wait_ge(hT_psum[0], pair)
                    act.activation(h1T[:], S[1][:], ACT.Relu).then_inc(hT_ready[0], 1)
                if t == L1["exp"]:
                    act.wait_ge(xh_psum, pair)
                    act.activation(exp1[:], V_bank[1][:], ACT.Exp, bias=cols[:, 0:1]).then_inc(xh_exp, 1)
                if t == L1["edge_copy"]:
                    act.wait_ge(edge_psum, pair)
                    act.activation(xh[:], V_bank[1][:].rearrange("p (r d) -> p r d", r=4), ACT.Copy).then_inc(xh_ready, 1)
                if t == L1["tanh"]:
                    act.wait_ge(src_ready, pair)
                    for y in range(2):
                        for r in range(NB):
                            n = NB * y + r
                            last = act.activation(edge[:, y, r], S[1][:, y * N:(y + 1) * N], ACT.Tanh,
                                                  bias=src_bias[:, n:n + 1], scale=0.5)
                    last.then_inc(edge_tanh, 1)
                if t == L1["agg_copy"]:
                    act.wait_ge(agg1_psum, pair)
                    act.activation(aggT[:], V_bank[1][:], ACT.Copy).then_inc(aggT_ready, 1)
                if t == L1["recv_exp"]:
                    act.wait_ge(recv_psum, pair)
                    act.activation(exp1r[:], V_bank[1][:], ACT.Exp, bias=cols[:, 1:2]).then_inc(recv_exp, 1)

            def layer2(t, turn):
                pair = turn.at(1, 0)
                if t == LN2["copy"]:
                    act.wait_ge(hT_psum[1], pair)
                    act.activation(h2T[:], V_bank[0][:], ACT.Relu).then_inc(hT_ready[1], 1)
                if t == L2["copy"]:
                    act.wait_ge(y_psum, pair)
                    act.activation(YT[:], S[0][:], ACT.Copy).then_inc(yT_ready, 1)
                if t == L2["tanh"]:
                    act.wait_ge(logit_psum, pair)
                    for y, bank_ in enumerate((S[0], V_bank[0])):
                        last = act.activation(logit2[:, y], bank_[:].rearrange("p (r n) -> p r n", r=NB), ACT.Tanh,
                                              scale=float(P) ** -0.5 / LOGIT_BOUND2)
                    last.then_inc(tanh2_ready, 1)
                if t == L2["exp"]:
                    act.wait_ge(tanh2_ready, pair)
                    act.activation(weight2[:], logit2[:], ACT.Exp, scale=LOGIT_BOUND2).then_inc(exp2_ready, 1)

            def layer3(t, turn):
                pair = turn.at(1, -1)
                if t == LN3["norm"]:
                    act.wait_ge(ln3_shift, pair)
                    for r in range(4):
                        last = act.activation(h3[:, r], X3_held[:, r], ACT.Relu, bias=shift3[:, r:r + 1], scale=rstd[:, 2, r:r + 1])
                    last.then_inc(h3_ready, 1)
                if t == LN3["copy"]:
                    act.wait_ge(hT_psum[2], pair)
                    act.activation(h3T[:], R0[:], ACT.Copy).then_inc(hT_ready[2], 1)
                s, p = divmod(t - L3_AT, L3_PERIOD)
                if not 0 <= s < STEPS:
                    return
                step = turn.at(STEPS, s + 1 - 2 * STEPS)
                if p == L3["copy"]:
                    act.wait_ge(m_psum, step)
                    act.activation(mT[:], R0[:], ACT.Copy).then_inc(mT_ready, 1)
                if p == L3["reset"]:
                    act.wait_ge(r_psum, step)
                    act.activation(tr[:], R1[:], ACT.Tanh, bias=bias3[:, 1:2], scale=0.5).then_inc(tr_ready, 1)
                if p == L3["z_gate"]:
                    act.wait_ge(z_psum, step)
                    act.activation(tz[:], R1[:], ACT.Tanh, bias=bias3[:, 0:1], scale=0.5).then_inc(tz_ready, 1)
                if p == L3["tanh"]:
                    act.wait_ge(cand_psum, step)
                    act.activation(cand[:], R0[:], ACT.Tanh, bias=bias3[:, 2:3]).then_inc(cand_ready, 1)
                if p == L3["back"] and s < STEPS - 1:
                    act.wait_ge(state_psum, step)
                    act.activation(h3[:], R1[:].rearrange("p (r d) -> p r d", r=4), ACT.Copy).then_inc(state_back, 1)

            act.wait_ge(dve_const, DVE_CONST_ALL)
            for p in sorted(PRE.values()):
                pre(p, 0, 1)

            def body(turn):
                for t in range(LOTS):
                    y, p = divmod(t, LOTS_B)
                    if turn.has_main:
                        blocks(turn, t)
                    if turn.has_post[y]:
                        post(p, 1 - y, turn.at(2, y))
                    if turn.has_main and (y == 0 or turn.pre_next):
                        pre(p, 1 - y, turn.at(2, y + 2))
                    if turn.has_l12:
                        layer1(t, turn)
                        layer2(t, turn)
                    if turn.has_l3:
                        layer3(t, turn)

            run_turns(act, body)

        @block.tensor
        def _(pe):
            def mm(dst, lhsT, rhs, start=True, stop=True):
                return pe.matmul(dst, lhsT, rhs, start=start, stop=stop)

            pe.wait_ge(gp_const, 2)
            pe.wait_ge(loaded, 16 * LOADS_COUNT)
            for j in range(NB):
                for i in range(NB):
                    last = pe.transpose(R0[:, j * N + i * P:j * N + (i + 1) * P], A[:, i, j * P:(j + 1) * P], ident[:])
            last.then_inc(pe_const, 1)
            for n, w in enumerate((raw2[:, 0], raw2[:, 1], rawu[:, 0], rawu[:, 1])):
                pe.transpose(R1[:, n * P:(n + 1) * P], w, ident[:])
            for n in range(3):
                for half in range(2):
                    last = mm(PB[:, n * P:(n + 1) * P], raw3[:, n, half * P:(half + 1) * P], ident[:], half == 0, half == 1)
            last.then_inc(pe_const, 1)
            pe.wait_ge(dve_const, DVE_CONST_TURNED)
            mm(R0[:, 0:P], qT, kT)
            for j in range(2):
                for c in range(EC):
                    mm(R1[:, j:j + 1], A[:, c, j * P:(j + 1) * P], a_lin[:, c:c + 1], c == 0, c == EC - 1)
            for c in range(EC):
                last = mm(R1[:, 2:3], a_lin_wide[:, c], b0_col[:, c:c + 1], c == 0, c == EC - 1)
            last.then_inc(pe_const, 1)
            pe.wait_ge(dve_const, DVE_CONST_ALL)

            def lot(turn, t):
                y, p = divmod(t, LOTS_B)
                row, c = divmod(p, EC)
                place, rnd = t % RING, t // RING
                if p == 0:
                    need(pe, prob_ready, turn.at(2, y - 1))
                    if y == 0:
                        need(pe, x3_ready, turn.at(1, -1))
                    elif turn.has_l12:
                        pe.wait_ge(x2_ready, turn.at(1, 0))
                    pe.wait_ge(h0T_ready, turn.at(2, y + 1))
                    pe.matmul(S[y][:].rearrange("p (r j) -> p r j", r=NB), w2_lin_wide[:],
                              H0T[:, y].unsqueeze(1).to_broadcast([P, NB, N]), start=True, stop=False,
                              skip_group_check=True)
                    pe.matmul(S[y][:].rearrange("p (r j) -> p r j", r=NB), ident[:], A_bias[:], start=False, stop=False,
                              skip_group_check=True)
                pe.wait_ge(by_dve[place], turn.at(ROUNDS, rnd + 1))
                pe.wait_ge(by_act[place], turn.at(ROUNDS, rnd + 1))
                for g in range(GROUPS):
                    last = pe.matmul(S[y][g * ROWS:(g + 1) * ROWS, :], a_window[:, c, ROWS - 1 - row:2 * ROWS - 1 - row],
                                     ring[:, place, g], start=False, stop=p == LOTS_B - 1, skip_group_check=True)
                last.then_inc(freed[place], 1)

            def pre(p, y, value, bank_read=None):
                if p == PRE["transpose"]:
                    pe.wait_ge(h0_ready, value)
                    for r in range(NB):
                        last = pe.transpose(PA[:, r * P:(r + 1) * P], H0[:, y, r], ident[:])
                    last.then_inc(h0T_psum, 1)
                if p == PRE["project"]:
                    pe.wait_ge(h0T_ready, value)
                    if bank_read is not None:
                        pe.wait_ge(*bank_read)
                    for r in range(NB):
                        mm(PA[:, N + r:N + r + 1], H0T[:, y, r * P:(r + 1) * P], w_lin[:, 0:1])
                    for j, bank_ in enumerate((PB, V_bank[y])):
                        for c in range(EC):
                            last = mm(bank_[:, c * N:(c + 1) * N], AT[:, j, c * P:(c + 1) * P], H0T[:, y])
                    last.then_inc(uv_psum, 1)

            def post(p, y, value):
                if p == POST["transpose"]:
                    pe.wait_ge(prob_ready, value)
                    for j in range(NB):
                        for i in range(NB):
                            last = pe.transpose(PB[:, j * N + i * P:j * N + (i + 1) * P], prob[:, i, j * P:(j + 1) * P], ident[:])
                    last.then_inc(probT_psum, 1)
                if p == POST["aggregate"]:
                    pe.wait_ge(probT_ready, value)
                    for i in range(NB):
                        for j in range(NB):
                            last = mm(PA[:, i * P:(i + 1) * P], probT[:, j, i * P:(i + 1) * P], H0[:, y, j], j == 0, j == NB - 1)
                    last.then_inc(attn_psum, 1)

            def turn_blocks(n, bank_):
                for r in range(4):
                    last = pe.transpose(bank_[:, r * P:(r + 1) * P], h3[:, r] if n == 2 else normed[:, n, r], ident[:])
                last.then_inc(hT_psum[n], 1)

            def layer1(t, turn):
                pair = turn.at(1, 0)
                if t == LN1["transpose"]:
                    pe.wait_ge(ln_normed[0], pair)
                    turn_blocks(0, S[1])
                if t == L1["project"]:
                    pe.wait_ge(hT_ready[0], pair)
                    mm(V_bank[1][:], Wi[:], h1T[:]).then_inc(xh_psum, 1)
                if t == L1["edge_terms"]:
                    pe.wait_ge(xhT_ready, pair)
                    mm(S[1][:], We_tgt_wide[:], xhT[:])
                    for n in range(4):
                        mm(PA[:, SRC_COLS.start + n:SRC_COLS.start + n + 1], xhT[:, n * P:(n + 1) * P], We[:, 0:1])
                    for n in range(4):
                        last = pe.transpose(V_bank[1][:, n * P:(n + 1) * P], xhT[:, n * P:(n + 1) * P], ident[:])
                    last.then_inc(edge_psum, 1)
                if t == L1["aggregate"]:
                    pe.wait_ge(xh_ready, pair)
                    pe.wait_ge(edge_ready, pair)
                    for y in range(2):
                        for r in range(NB):
                            mm(V_bank[1][:, y * N:(y + 1) * N], xh[:, NB * y + r], edge[:, y, r], r == 0, r == NB - 1)
                    for y in range(2):
                        for r in range(NB):
                            last = mm(S[1][:, y * N:(y + 1) * N], ones[:], edge[:, y, r], r == 0, r == NB - 1)
                    last.then_inc(agg1_psum, 1)
                if t == L1["receive"]:
                    pe.wait_ge(aggT_ready, pair)
                    mm(V_bank[1][:], Wn[:, 0], aggT[:], True, False)
                    pe.wait_ge(selfT_ready, pair)
                    mm(V_bank[1][:], Wn[:, 1], selfT[:], False, True).then_inc(recv_psum, 1)
                if t == L1["out"]:
                    pe.wait_ge(recvT_ready, pair)
                    for n in range(4):
                        mm(S[1][:, n * P:(n + 1) * P], ones[0:1, :], bm_half[:], True, False)
                        mm(S[1][:, n * P:(n + 1) * P], recvT[:, n * P:(n + 1) * P], Wm[:, 0], False, False)
                        last = mm(S[1][:, n * P:(n + 1) * P], xhT[:, n * P:(n + 1) * P], Wm[:, 1], False, True)
                    last.then_inc(out1_psum, 1)

            def layer2(t, turn):
                pair = turn.at(1, 0)
                if t == LN2["transpose"]:
                    pe.wait_ge(ln_normed[1], pair)
                    turn_blocks(1, V_bank[0])
                if t == L2["project"]:
                    pe.wait_ge(hT_ready[1], pair)
                    pe.wait_ge(prob_ready, turn.at(2, 1 if turn.has_main else 0))
                    mm(S[0][:], G[:], h2T[:])
                    for n in range(4):
                        last = mm(V_bank[0][:, n * P:(n + 1) * P], h2T[:, n * P:(n + 1) * P], Wv[:])
                    last.then_inc(y_psum, 1)
                if t == L2["scores"]:
                    pe.wait_ge(yT_ready, pair)
                    pe.wait_ge(hv_ready, pair)
                    for y, bank_ in enumerate((S[0], V_bank[0])):
                        for r in range(NB):
                            n = NB * y + r
                            last = mm(bank_[:, r * N:(r + 1) * N], h2T[:, n * P:(n + 1) * P], YT[:, y * N:(y + 1) * N])
                    last.then_inc(logit_psum, 1)
                if t == L2["aggregate"]:
                    pe.wait_ge(weight2_ready, pair)
                    for y, bank_ in enumerate((S[0], V_bank[0])):
                        for i in range(NB):
                            for r in range(NB):
                                last = mm(bank_[:, i * (P + 1):(i + 1) * (P + 1)], weight2[:, y, r, i * P:(i + 1) * P],
                                          HV[:, NB * y + r], r == 0, r == NB - 1)
                    last.then_inc(agg2_psum, 1)

            def layer3(t, turn):
                pair = turn.at(1, -1)
                if t == LN3["transpose"]:
                    pe.wait_ge(h3_ready, pair)
                    turn_blocks(2, R0)
                s, p = divmod(t - L3_AT, L3_PERIOD)
                if not 0 <= s < STEPS:
                    return
                step = turn.at(STEPS, s + 1 - 2 * STEPS)
                if p == L3["message"]:
                    if s == 0:
                        pe.wait_ge(hT_ready[2], pair)
                    else:
                        pe.wait_ge(state_back, turn.at(STEPS - 1, s - 2 * (STEPS - 1)))
                    for y in range(2):
                        for r in range(NB):
                            last = mm(R0[:, y * N:(y + 1) * N], h3[:, NB * y + r], AT[:, r], r == 0, r == NB - 1)
                    last.then_inc(m_psum, 1)
                if p == L3["gates"]:
                    pe.wait_ge(mT_ready, step)
                    mm(R1[:], W345[:, 1], mT[:], True, False)
                    mm(R1[:], u3T, h3T[:], False, True).then_inc(r_psum, 1)
                    mm(R0[:], W345[:, 2], mT[:], True, False)
                if p == L3["candidate"]:
                    pe.wait_ge(tr_ready, step)
                    pe.matmul(R1[:], W345[:, 0], mT[:], start=False, stop=True, skip_group_check=True).then_inc(z_psum, 1)
                    pe.wait_ge(rh_ready, step)
                    mm(R0[:], u5T_half, rh[:], False, True).then_inc(cand_psum, 1)
                if p == L3["transpose"]:
                    pe.wait_ge(state_ready, step)
                    pe.wait_ge(tz_ready, step)
                    for n in range(4):
                        last = pe.transpose(R1[:, n * P:(n + 1) * P], h3T[:, n * P:(n + 1) * P], ident[:])
                    last.then_inc(state_psum, 1)

            for p in sorted(PRE.values()):
                pre(p, 0, 1)

            def body(turn):
                for t in range(LOTS):
                    if turn.has_main:
                        lot(turn, t)
                    t += LEAD
                    if t >= LOTS:
                        continue
                    y, p = divmod(t, LOTS_B)
                    if turn.has_post[y]:
                        post(p, 1 - y, turn.at(2, y))
                    if turn.has_main and (y == 0 or turn.pre_next):
                        pre(p, 1 - y, turn.at(2, y + 2), (x3_ready if y else recvT_ready, turn.at(1, 0)) if turn.has_l12 else None)
                    if turn.has_l12:
                        layer1(t, turn)
                        layer2(t, turn)
                    if turn.has_l3:
                        layer3(t, turn)

            run_turns(pe, body)


_INS = ["x", "adj", "L0_gnn_b_lin", "L0_gnn_a", "L1_gnn_Wi", "L1_gnn_bi", "L1_gnn_We", "L1_gnn_be", "L1_gnn_Wn",
        "L1_gnn_bn", "L1_gnn_Wm", "L1_gnn_bm", "L2_gnn_q", "L2_gnn_k", "L2_gnn_v", "L3_gnn_w3_w", "L3_gnn_w3_b",
        "L3_gnn_u3_w", "L3_gnn_u3_b", "L3_gnn_w4_w", "L3_gnn_w4_b", "L3_gnn_w5_w", "L3_gnn_w5_b", "L3_gnn_u5_w",
        "L3_gnn_u5_b"]


def kernel(**inputs):
    import numpy as np
    import concourse.bacc as bacc
    from concourse.bass_utils import run_bass_kernel_spmd

    nc = bacc.Bacc("TRN2", target_bir_lowering=False, num_devices=1)
    arrays, args = {}, []
    for name in _INS:
        a = np.ascontiguousarray(inputs[name])
        arrays[f"in_{name}"] = a
        args.append(nc.dram_tensor(f"in_{name}", a.shape, mybir.dt.from_np(a.dtype), kind="ExternalInput").ap())
    out = nc.dram_tensor("out", inputs["x"].shape, F32, kind="ExternalOutput").ap()
    gnn_stack(nc, *args, out)
    results = run_bass_kernel_spmd(nc, [arrays], core_ids=[0])
    return results.results[0]["out"]
```

```python
from contextlib import ExitStack

import concourse.bass as bass
from concourse import mybir

F32 = mybir.dt.float32
ALU = mybir.AluOpType
ACT = mybir.ActivationFunctionType
AXIS = mybir.AxisListType

P = 128
N = 256
NB = N // P
E = 256
EC = E // P
NEG_SLOPE0 = 0.2
MASK_ALPHA1 = 0.005
LN_EPS = 1e-5
STEPS = 5
LOGIT_BOUND2 = 8.0

GROUPS = 4
ROWS = P // GROUPS
LOTS_B = EC * ROWS
LOTS = 2 * LOTS_B
BLOCKS = GROUPS * NB
RING = 8
ROUNDS = LOTS // RING

LEAD = 3
POST = dict(score=5, exp=6, transpose=10, copy=11, aggregate=12, tanh=14, residual=15)
PRE = dict(stats=40, norm=43, transpose=46, copy=49, project=57, evacuate=61)
LN1 = dict(stats=17, norm=19, transpose=20, copy=23)
L1 = dict(project=26, exp=28, elu=29, edge_terms=31, edge_copy=33, tanh=33, mask=36, aggregate=39, agg_copy=42,
          receive=44, recv_exp=45, recv_elu=47, out=49, residual=52)
LN2 = dict(stats=56, norm=59, transpose=68, copy=70)
L2 = dict(project=74, copy=77, scores=80, tanh=84, exp=85, mask=88, aggregate=94, residual=99)
LN3 = dict(stats=2, norm=5, transpose=9, copy=10)
L3_AT, L3_PERIOD = 12, 22
L3 = dict(message=0, copy=2, gates=4, reset=7, update=9, candidate=10, z_gate=12, tanh=13, state=15, transpose=18, back=20)

SRC_COLS = slice(2 * N - 4, 2 * N)
LOADS0, LOADS_REST = 3, 21
SETUP_REST = dict(vector_raw=12, transpose=14, vector_turned=20, product=24, vector_product=30, ready=34)
DVE_CONST_A_LIN, DVE_CONST_ALL = 4, 7
DVE_REST_TURNED, DVE_REST_ALL = 6, 7

VECTOR_BLOCK, SCALAR_BLOCK = 2.63, 3.62


def stage_costs():
    vector, scalar = [0.0] * LOTS, [0.0] * LOTS

    def put(costs, table, at, **stages):
        for name, cost in stages.items():
            costs[at + table[name]] += cost

    for half in (0, LOTS_B):
        put(vector, POST, half, score=7, transpose=1.5, residual=3.4)
        put(scalar, POST, half, exp=10, copy=4.8, tanh=5)
        put(vector, PRE, half, stats=5.5, evacuate=0.6)
        put(scalar, PRE, half, norm=5, copy=2.6, evacuate=12)
    for ln in (LN1, LN2, LN3):
        put(vector, ln, 0, stats=11)
        put(scalar, ln, 0, norm=10, copy=4.8)
    put(vector, L1, 0, elu=10, edge_copy=1.3, mask=12, agg_copy=6, recv_elu=10, residual=6)
    put(scalar, L1, 0, exp=5.7, edge_copy=4.8, tanh=14.2, agg_copy=4.8, recv_exp=5.7)
    put(vector, L2, 0, mask=11.4, residual=11.8)
    put(scalar, L2, 0, copy=9.6, tanh=9.6, exp=9.5)
    for s in range(STEPS):
        put(vector, L3, L3_AT + s * L3_PERIOD, update=6, state=18)
        put(scalar, L3, L3_AT + s * L3_PERIOD, copy=4.8, reset=5.7, z_gate=5.7, tanh=5.7, back=4.8 if s < STEPS - 1 else 0)
    return vector, scalar


def share_blocks():
    vector, scalar = stage_costs()
    shares, v, s = [], 0.0, 0.0
    for t in range(LOTS):
        n = min(range(1, BLOCKS), key=lambda n: max(v + (BLOCKS - n) * VECTOR_BLOCK, s + n * SCALAR_BLOCK))
        shares.append(n)
        v += (BLOCKS - n) * VECTOR_BLOCK + vector[t]
        s += n * SCALAR_BLOCK + scalar[t]
    return shares


ACT_BLOCKS = share_blocks()


def spare_blocks():
    spare = [0] * LOTS
    for half in (0, LOTS_B):
        for at in (POST["score"], POST["transpose"], PRE["stats"]):
            spare[half + at] += 1
    for at in (LN1["stats"], LN2["stats"], LN3["stats"], L1["elu"], L1["recv_elu"], L2["residual"]):
        spare[at] += 1
    for s in range(STEPS):
        spare[L3_AT + s * L3_PERIOD + L3["state"]] += 2
    return spare


SPARE_BLOCKS = spare_blocks()


def gnn_stack(nc, x, adj, L0_b, L0_a, L1_Wi, L1_bi, L1_We, L1_be, L1_Wn, L1_bn, L1_Wm, L1_bm, L2_q, L2_k, L2_v,
              L3_w3_w, L3_w3_b, L3_u3_w, L3_u3_b, L3_w4_w, L3_w4_b, L3_w5_w, L3_w5_b, L3_u5_w, L3_u5_b, out):
    BATCHES = x.shape[0]
    PAIRS = BATCHES // 2
    x_rows = x.rearrange("b (r p) d -> b p r d", p=P)
    out_rows = out.rearrange("b (r p) d -> b p r d", p=P)

    class Turn:

        def __init__(self, m=None, it=None):
            self.m, self.it = m, it
            self.has_main = it is not None or m < PAIRS
            self.has_post = [it is not None or 1 <= m <= PAIRS, self.has_main]
            self.has_l12 = it is not None or 1 <= m <= PAIRS
            self.has_l3 = it is not None or m >= 2
            self.pre_next = it is not None or m < PAIRS - 1

        def at(self, per_turn, more):
            if self.it is None:
                return per_turn * self.m + more
            return self.it * per_turn + (2 * per_turn + more)

    def need(eng, sem, value):
        if isinstance(value, int) and value <= 0:
            return
        eng.wait_ge(sem, value)

    def run_turns(eng, body):
        for m in range(2):
            body(Turn(m=m))
        with eng.Fori(0, PAIRS - 3) as it:
            body(Turn(it=it))
        for m in range(PAIRS - 1, PAIRS + 2):
            body(Turn(m=m))

    with ExitStack() as ctx:
        def sb(name, shape):
            return ctx.enter_context(nc.sbuf_tensor(name, shape, F32))

        def bank(name):
            return ctx.enter_context(nc.psum_tensor(name, [P, 512], F32))

        def sem(name):
            return ctx.enter_context(nc.semaphore(name))

        def sems(names):
            return [sem(n) for n in names.split()]

        ident = sb("ident", [P, P])
        ones = sb("ones", [P, P])
        eps = sb("eps", [P, 4])
        minus_one = sb("minus_one", [P, 4])
        minus_half = sb("minus_half", [P, 4])
        A = sb("A", [P, NB, N])
        AT = sb("AT", [P, NB, N])
        a_col = sb("a_col", [P, EC])
        a_lin = sb("a_lin", [P, EC])
        a_lin_wide = sb("a_lin_wide", [P, EC, P])
        a_window = sb("a_window", [P, EC, 2 * ROWS - 1])
        b0_col = sb("b0_col", [P, EC])
        w_lin = sb("w_lin", [P, 3])
        w2_lin_wide = sb("w2_lin_wide", [P, P])
        A_bias = sb("A_bias", [P, NB, N])
        maskT = sb("maskT", [P, NB, N])
        maskT_tmp = sb("maskT_tmp", [P, NB, N])
        Wi = sb("Wi", [P, P])
        We = sb("We", [P, 2])
        be = sb("be", [P, 1])
        We_tgt_wide = sb("We_tgt_wide", [P, P])
        Wn = sb("Wn", [P, 2, P])
        Wm = sb("Wm", [P, 2, P])
        bm_half = sb("bm_half", [1, P])
        cols = sb("cols", [P, 7])
        bias3 = sb("bias3", [P, 3])
        raw2 = sb("raw2", [P, 2, P])
        Wv = sb("Wv", [P, P])
        raw3 = sb("raw3", [P, 3, 2 * P])
        rawu = sb("rawu", [P, 2, P])
        turned = sb("turned", [P, 4, P])
        G = sb("G", [P, P])
        W345 = sb("W345", [P, 3, P])
        qT, kT, u3T, u5T_half = (turned[:, n, :] for n in range(4))

        X0 = sb("X0", [P, 2, NB, P])
        H0 = sb("H0", [P, 2, NB, P])
        H0T = sb("H0T", [P, 2, N])
        U = sb("U", [P, 2, EC, N])
        V = sb("V", [P, 2, EC, N])
        lin_i = sb("lin_i", [P, 2, NB])
        ring = sb("ring", [P, RING, GROUPS, NB * N])
        st0 = sb("st0", [P, NB, 6])
        mv0 = sb("mv0", [P, NB, 2])
        var0 = sb("var0", [P, NB])
        rstd0 = sb("rstd0", [P, NB])
        minus_mean0 = sb("minus_mean0", [P, NB])
        shift0 = sb("shift0", [P, NB])
        prob = sb("prob", [P, NB, N])
        probT = sb("probT", [P, NB, N])
        neg_max = sb("neg_max", [P, NB])
        exp_bias = sb("exp_bias", [P, NB])
        row_sum = sb("row_sum", [P, NB])
        inv_sum = sb("inv_sum", [P, NB])
        half_inv = sb("half_inv", [P, NB])
        tanh0 = sb("tanh0", [P, NB, P])

        X1 = sb("X1", [P, 4, P])
        X2 = sb("X2", [P, 4, P])
        X3 = sb("X3", [P, 4, P])
        X3_held = sb("X3_held", [P, 4, P])
        OUT = sb("OUT", [P, 4, P])
        st = sb("st", [P, 3, 4, 6])
        wait_carrier = sb("wait_carrier", [P, 1])
        mv = sb("mv", [P, 3, 4, 2])
        var = sb("var", [P, 3, 4])
        rstd = sb("rstd", [P, 3, 4])
        minus_mean = sb("minus_mean", [P, 3, 4])
        shift = sb("shift", [P, 3, 4])
        h1 = sb("h1", [P, 4, P])
        h2 = sb("h2", [P, 4, P])
        h1T = sb("h1T", [P, 2 * N])
        exp1 = sb("exp1", [P, 2 * N])
        xhT = sb("xhT", [P, 2 * N])
        xh = sb("xh", [P, 4, P])
        src_bias = sb("src_bias", [P, 4])
        edge = sb("edge", [P, 2, NB, N])
        aggT = sb("aggT", [P, 2 * N])
        selfT = sb("selfT", [P, 2 * N])
        exp1r = sb("exp1r", [P, 2 * N])
        recvT = sb("recvT", [P, 2 * N])
        h2T = sb("h2T", [P, 2 * N])
        YT = sb("YT", [P, 2 * N])
        HV = sb("HV", [P, 4, P + 1])
        logit2 = sb("logit2", [P, 2, NB, N])
        weight2 = sb("weight2", [P, 2, NB, N])
        inv2 = sb("inv2", [P, 4])
        h3T = sb("h3T", [P, 2 * N])
        h3 = sb("h3", [P, 4, P])
        mT = sb("mT", [P, 2 * N])
        tr = sb("tr", [P, 2 * N])
        tz = sb("tz", [P, 2 * N])
        rh = sb("rh", [P, 2 * N])
        cand = sb("cand", [P, 2 * N])
        diff = sb("diff", [P, 2 * N])
        gated = sb("gated", [P, 2 * N])

        S = [bank("S0"), bank("S1")]
        V_bank = [bank("V0"), bank("V1")]
        PA, PB = bank("PA"), bank("PB")
        R0, R1 = bank("R0"), bank("R1")

        loaded = sem("loaded")
        gp_const, dve_const, pe_const = sem("gp_const"), sem("dve_const"), sem("pe_const")
        loaded_rest, dve_rest_const, pe_rest_const = sem("loaded_rest"), sem("dve_rest_const"), sem("pe_rest_const")
        by_dve = [sem(f"by_dve{n}") for n in range(RING)]
        by_act = [sem(f"by_act{n}") for n in range(RING)]
        freed = [sem(f"freed{n}") for n in range(RING)]
        x_loaded, pre_stats, pre_mv, pre_eps, pre_rstd = sems("x_loaded pre_stats pre_mv pre_eps pre_rstd")
        pre_shift, h0_ready, h0T_psum, h0T_ready = sems("pre_shift h0_ready h0T_psum h0T_ready")
        uv_psum, u_ready, v_ready = sems("uv_psum u_ready v_ready")
        max_ready, exp_bias_ready, prob_ready = sems("max_ready exp_bias_ready prob_ready")
        probT_psum, probT_ready, inv_ready, half_inv_ready = sems("probT_psum probT_ready inv_ready half_inv_ready")
        attn_psum, tanh0_ready, x1_ready = sems("attn_psum tanh0_ready x1_ready")
        ln_stats = [sem(f"ln{n}_stats") for n in (1, 2, 3)]
        ln_mv = [sem(f"ln{n}_mv") for n in (1, 2, 3)]
        ln_eps = [sem(f"ln{n}_eps") for n in (1, 2, 3)]
        ln_rstd = [sem(f"ln{n}_rstd") for n in (1, 2, 3)]
        ln_shift = [sem(f"ln{n}_shift") for n in (1, 2, 3)]
        h_ready = [sem(f"h{n}_ready") for n in (1, 2, 3)]
        hT_psum = [sem(f"h{n}T_psum") for n in (1, 2, 3)]
        hT_ready = [sem(f"h{n}T_ready") for n in (1, 2, 3)]
        xh_psum, xh_exp, xh_min, xhT_ready = sems("xh_psum xh_exp xh_min xhT_ready")
        edge_psum, src_ready, xh_ready, edge_tanh, edge_ready = sems("edge_psum src_ready xh_ready edge_tanh edge_ready")
        agg1_psum, aggT_ready, selfT_ready = sems("agg1_psum aggT_ready selfT_ready")
        recv_psum, recv_exp, recv_min, recvT_ready = sems("recv_psum recv_exp recv_min recvT_ready")
        out1_psum, x2_ready = sem("out1_psum"), sem("x2_ready")
        y_psum, yT_ready, hv_ready, logit_psum, tanh2_ready = sems("y_psum yT_ready hv_ready logit_psum tanh2_ready")
        exp2_ready, weight2_ready, agg2_psum, inv2_ready, x3_ready = sems("exp2_ready weight2_ready agg2_psum inv2_ready x3_ready")
        x3_held = sem("x3_held")
        m_psum, mT_ready, r_psum, tr_ready, rh_ready, z_psum, tz_ready = sems("m_psum mT_ready r_psum tr_ready rh_ready z_psum tz_ready")
        cand_psum, cand_ready, diff_ready, gated_ready = sems("cand_psum cand_ready diff_ready gated_ready")
        state_ready, state_psum, state_back = sems("state_ready state_psum state_back")
        out_ready, out_stored = sem("out_ready"), sem("out_stored")

        def layer3_parts(turn, s):
            if turn.it is not None or turn.m <= PAIRS:
                return [(slice(0, 2 * N), slice(0, 2 * NB), R0, R1, turn.at(STEPS, s + 1 - 2 * STEPS),
                         turn.at(STEPS - 1, s - 2 * (STEPS - 1)))]
            return [(slice(y * N, (y + 1) * N), slice(y * NB, (y + 1) * NB), (R0, S[0])[y], (R1, S[1])[y],
                     STEPS * (PAIRS - 1) + 2 * s + y + 1, (STEPS - 1) * (PAIRS - 1) + 2 * s + y - 1) for y in range(2)]

        def rows(ap):
            return ap.rearrange("p (r d) -> p r d", d=P)

        block = ctx.enter_context(nc.Block())

        @block.sync
        def _(sp):
            def load(dst, src, done=loaded_rest):
                sp.dma_start(dst, src, allow_slow_non_contiguous=True).then_inc(done, 16)

            sp.sem_inc(out_stored, 16)
            sp.dma_start(X0[:, 0], x_rows[0]).then_inc(x_loaded, 16)
            load(A[:], adj.rearrange("(r p) j -> p r j", p=P), loaded)
            load(a_col[:], L0_a.rearrange("(c p) -> p c", p=P), loaded)
            load(b0_col[:], L0_b.rearrange("(c p) -> p c", p=P), loaded)
            load(Wi[:], L1_Wi)
            load(We[:], L1_We.rearrange("(c p) o -> p (c o)", p=P))
            load(be[:], L1_be.partition_broadcast(P))
            load(Wn[:], L1_Wn.rearrange("(c p) o -> p c o", p=P))
            load(Wm[:], L1_Wm.rearrange("(c p) o -> p c o", p=P))
            load(bm_half[:], L1_bm.rearrange("(o d) -> o d", o=1))
            for n, b in enumerate((L1_bi, L1_bn, L3_w3_b, L3_w4_b, L3_w5_b, L3_u3_b, L3_u5_b)):
                load(cols[:, n:n + 1], b.rearrange("(p o) -> p o", o=1))
            load(raw2[:, 0], L2_q)
            load(raw2[:, 1], L2_k)
            load(Wv[:], L2_v)
            for n, w in enumerate((L3_w3_w, L3_w4_w, L3_w5_w)):
                load(raw3[:, n], w)
            load(rawu[:, 0], L3_u3_w)
            load(rawu[:, 1], L3_u5_w)

            def body(turn):
                for y in range(2):
                    if turn.has_main and (y == 0 or turn.pre_next):
                        need(sp, x1_ready, turn.at(2, y))
                        if turn.m == 0 and y == 0:
                            sp.wait_ge(pre_stats, 1)
                        b = turn.at(2, y + 1)
                        sp.dma_start(X0[:, 1 - y], x_rows[b] if isinstance(b, int) else x_rows[bass.ds(b, 1)].rearrange("o p r d -> (o p) r d")).then_inc(x_loaded, 16)
                if turn.has_l3:
                    sp.wait_ge(out_ready, turn.at(1, -1))
                    for y in range(2):
                        if turn.m == PAIRS + 1 and y == 1:
                            sp.wait_ge(out_ready, PAIRS + 1)
                        b = turn.at(2, y - 4)
                        dst = out_rows[b] if isinstance(b, int) else out_rows[bass.ds(b, 1)].rearrange("o p r d -> (o p) r d")
                        sp.dma_start(dst, OUT[:, NB * y:NB * y + NB]).then_inc(out_stored, 16)
                if turn.has_l12:
                    sp.wait_ge(x3_ready, turn.at(1, 0))
                    sp.dma_start(X3_held[:], X3[:]).then_inc(x3_held, 16)

            run_turns(sp, body)
            sp.wait_ge(out_stored, 16 * (BATCHES + 1))

        @block.gpsimd
        def _(gp):
            gp.memset(ident[:], 0.0).then_inc(gp_const, 1)
            gp.wait_ge(gp_const, 1)
            gp.affine_select(out=ident[:], in_=ident[:], compare_op=ALU.not_equal, fill=1.0, base=0,
                             pattern=[[-1, P]], channel_multiplier=1).then_inc(gp_const, 1)
            gp.wait_ge(dve_const, 1)

            def norm_factors(mean, var_, eps_var, rstd_, minus_mean_, shift_, width, sem_in, sem_eps, sem_rstd, sem_shift, value):
                gp.wait_ge(sem_in, value)
                gp.tensor_tensor(minus_mean_, mean, minus_one[:, 0:width], ALU.mult)
                gp.tensor_tensor(eps_var, var_, eps[:, 0:width], ALU.add).then_inc(sem_eps, 1)
                gp.wait_ge(sem_eps, value)
                gp.tensor_tensor(rstd_, eps_var, minus_half[:, 0:width], ALU.pow).then_inc(sem_rstd, 1)
                gp.wait_ge(sem_rstd, value)
                gp.tensor_tensor(shift_, minus_mean_, rstd_, ALU.mult).then_inc(sem_shift, 1)

            def pre(value):
                norm_factors(mv0[:, :, 0], mv0[:, :, 1], var0[:], rstd0[:], minus_mean0[:], shift0[:], NB,
                             pre_mv, pre_eps, pre_rstd, pre_shift, value)

            def norm(n, turn):
                norm_factors(mv[:, n, :, 0], mv[:, n, :, 1], var[:, n], rstd[:, n], minus_mean[:, n], shift[:, n], 4,
                             ln_mv[n], ln_eps[n], ln_rstd[n], ln_shift[n], turn.at(1, -(n // 2)))

            pre(1)

            def body(turn):
                for t in range(LOTS):
                    y, p = divmod(t, LOTS_B)
                    if p == PRE["stats"] and turn.has_main and (y == 0 or turn.pre_next):
                        pre(turn.at(2, y + 2))
                    for n, (ln, runs) in enumerate(((LN1, turn.has_l12), (LN2, turn.has_l12), (LN3, turn.has_l3))):
                        if t == ln["stats"] and runs:
                            norm(n, turn)

            run_turns(gp, body)

        @block.vector
        def _(dve):
            def constant(ins, step, done=dve_const):
                ins.then_inc(done, 1)
                dve.wait_ge(done, step)

            def setup_layer0():
                constant(dve.memset(a_window[:], 0.0), 2)
                dve.wait_ge(loaded, 16 * LOADS0)
                dve.tensor_scalar(a_window[:, :, ROWS - 1:ROWS], a_col[:].unsqueeze(2), 1.0 - NEG_SLOPE0, None, ALU.mult)
                constant(dve.tensor_scalar(a_lin[:], a_col[:], NEG_SLOPE0, None, ALU.mult), 3)
                constant(dve.tensor_copy(a_lin_wide[:], a_lin[:].unsqueeze(2).to_broadcast([P, EC, P])), DVE_CONST_A_LIN)
                dve.wait_ge(pe_const, 1)
                constant(dve.tensor_copy(AT[:], R0[:].rearrange("p (r i) -> p r i", r=NB)), 5)
                dve.wait_ge(pe_const, 2)
                constant(dve.tensor_copy(w_lin[:], R1[:, 0:3]), 6)
                dve.tensor_copy(w2_lin_wide[:], w_lin[:, 1:2].to_broadcast([P, P]))
                constant(dve.tensor_scalar(A_bias[:], A[:], w_lin[:, 2:3], None, ALU.add), DVE_CONST_ALL)

            def setup_rest(t):
                if t == SETUP_REST["vector_raw"]:
                    dve.wait_ge(loaded_rest, 16 * LOADS_REST)
                    dve.memset(ones[:], 1.0)
                    dve.memset(HV[:, :, P:P + 1], 1.0)
                    dve.tensor_copy(We_tgt_wide[:], We[:, 1:2].to_broadcast([P, P]))
                    dve.tensor_scalar(bm_half[:], bm_half[:], 0.5, None, ALU.add)
                    dve.tensor_tensor(bias3[:, 0:2], cols[:, 2:4], cols[:, 5:6].to_broadcast([P, 2]), ALU.add)
                    constant(dve.tensor_tensor(bias3[:, 2:3], cols[:, 4:5], cols[:, 6:7], ALU.add), 1, dve_rest_const)
                    constant(dve.tensor_scalar(bias3[:, 0:2], bias3[:, 0:2], 0.5, None, ALU.mult), 2, dve_rest_const)
                    constant(dve.tensor_scalar(maskT_tmp[:], AT[:], 0.0, -0.5 * MASK_ALPHA1, ALU.not_equal, ALU.mult), 3, dve_rest_const)
                    constant(dve.tensor_scalar(maskT_tmp[:], maskT_tmp[:], 0.5 * MASK_ALPHA1, None, ALU.add), 4, dve_rest_const)
                    dve.scalar_tensor_tensor(maskT[:], AT[:], 0.5, maskT_tmp[:], ALU.mult, ALU.add)
                if t == SETUP_REST["vector_turned"]:
                    dve.wait_ge(pe_rest_const, 1)
                    dve.tensor_copy(turned[:, 0:3], R1[:, 0:3 * P].rearrange("p (n k) -> p n k", n=3))
                    dve.tensor_scalar(turned[:, 3], R1[:, 3 * P:4 * P], 0.5, None, ALU.mult)
                    constant(dve.tensor_copy(W345[:], R0[:, 0:3 * P].rearrange("p (n k) -> p n k", n=3)), 5, dve_rest_const)
                    constant(dve.tensor_tensor(W345[:, 0], W345[:, 0], W345[:, 1], ALU.subtract), DVE_REST_TURNED, dve_rest_const)
                if t == SETUP_REST["vector_product"]:
                    dve.wait_ge(pe_rest_const, 2)
                    constant(dve.tensor_copy(G[:], R0[:, 0:P]), DVE_REST_ALL, dve_rest_const)

            lot = dict(blocks=0, done=0)

            def start_lot(turn, t):
                lot.update(turn=turn, t=t, blocks=BLOCKS - ACT_BLOCKS[t], done=0)
                need(dve, freed[t % RING], turn.at(ROUNDS, t // RING))
                if t % LOTS_B == 0:
                    y = t // LOTS_B
                    dve.wait_ge(u_ready, turn.at(2, y + 1))
                    dve.wait_ge(v_ready, turn.at(2, y + 1))
                while lot["done"] < max(1, lot["blocks"] - SPARE_BLOCKS[t]):
                    one_block()

            def one_block():
                if lot["done"] == lot["blocks"]:
                    return
                y, p = divmod(lot["t"], LOTS_B)
                row, c = divmod(p, EC)
                place = lot["t"] % RING
                g, half = divmod(lot["done"], NB)
                i = half * P + g * ROWS + row
                block_ = dve.tensor_scalar(ring[:, place, g, half * N:(half + 1) * N], V[:, y, c],
                                           U[:, y, c, i:i + 1], 0.0, ALU.add, ALU.max)
                lot["done"] += 1
                if lot["done"] == lot["blocks"]:
                    block_.then_inc(by_dve[place], 1)

            def finish_lot():
                while lot["done"] < lot["blocks"]:
                    one_block()

            def pre(p, y, value):
                if p == PRE["stats"]:
                    dve.wait_ge(x_loaded, value * 16)
                    for r in range(NB):
                        last = dve.bn_stats(st0[:, r], X0[:, y, r])
                    last.then_inc(pre_stats, 1)
                    one_block()
                    dve.wait_ge(pre_stats, value)
                    dve.memset(wait_carrier[:], 0.0)
                    for r in range(NB):
                        last = dve.bn_aggr(mv0[:, r], st0[:, r])
                    last.then_inc(pre_mv, 1)
                if p == PRE["evacuate"]:
                    dve.wait_ge(uv_psum, value)
                    dve.tensor_copy(lin_i[:, y], PA[:, N:N + NB])

            def post(p, y, value, lots_done):
                if p == POST["score"]:
                    dve.wait_ge(freed[RING - 1], lots_done)
                    dve.tensor_reduce(neg_max[:], S[y][:].rearrange("p (r j) -> p r j", r=NB), AXIS.X, ALU.max,
                                      negate=True).then_inc(max_ready, 1)
                    one_block()
                    dve.wait_ge(max_ready, value)
                    for r in range(NB):
                        last = dve.scalar_tensor_tensor(exp_bias[:, r:r + 1], neg_max[:, r:r + 1], lin_i[:, y, r:r + 1],
                                                        lin_i[:, y, r:r + 1], ALU.subtract, ALU.add)
                    last.then_inc(exp_bias_ready, 1)
                if p == POST["transpose"]:
                    dve.wait_ge(prob_ready, value)
                    dve.reciprocal(inv_sum[:], row_sum[:]).then_inc(inv_ready, 1)
                    one_block()
                    dve.wait_ge(inv_ready, value)
                    dve.tensor_scalar(half_inv[:], inv_sum[:], 0.5, None, ALU.mult).then_inc(half_inv_ready, 1)
                if p == POST["residual"]:
                    dve.wait_ge(tanh0_ready, value)
                    dve.scalar_tensor_tensor(X1[:, NB * y:NB * y + NB], tanh0[:], 0.5, X0[:, y], ALU.mult,
                                             ALU.add).then_inc(x1_ready, 1)

            def stats(t, ln, n, src, pair):
                if t == ln["stats"]:
                    for r in range(4):
                        last = dve.bn_stats(st[:, n, r], src[:, r])
                    last.then_inc(ln_stats[n], 1)
                    one_block()
                    dve.wait_ge(ln_stats[n], pair)
                    dve.memset(wait_carrier[:], 0.0)
                    for r in range(4):
                        last = dve.bn_aggr(mv[:, n, r], st[:, n, r])
                    last.then_inc(ln_mv[n], 1)

            def elu(bank_, bias, exp_, dst, sem_exp, sem_min, sem_out, turn):
                dve.wait_ge(sem_exp, turn.at(1, 0))
                dve.tensor_scalar(exp_[:], exp_[:], 1.0, 1.0, ALU.min, ALU.subtract).then_inc(sem_min, 1)
                one_block()
                dve.wait_ge(sem_min, turn.at(1, 0))
                dve.scalar_tensor_tensor(dst[:], bank_[:], bias, exp_[:], ALU.add, ALU.max).then_inc(sem_out, 1)

            def layer1(t, turn):
                pair = turn.at(1, 0)
                if t == LN1["stats"]:
                    dve.wait_ge(x1_ready, turn.at(2, 0))
                stats(t, LN1, 0, X1, pair)
                if t == L1["elu"]:
                    elu(V_bank[1], cols[:, 0:1], exp1, xhT, xh_exp, xh_min, xhT_ready, turn)
                if t == L1["edge_copy"]:
                    dve.wait_ge(edge_psum, pair)
                    dve.tensor_scalar(src_bias[:], PA[:, SRC_COLS], be[:], 0.5, ALU.add, ALU.mult).then_inc(src_ready, 1)
                if t == L1["mask"]:
                    dve.wait_ge(edge_tanh, pair)
                    for y in range(2):
                        last = dve.scalar_tensor_tensor(edge[:, y], edge[:, y], 1.0, maskT[:], ALU.add, ALU.mult)
                    last.then_inc(edge_ready, 1)
                if t == L1["agg_copy"]:
                    dve.wait_ge(agg1_psum, pair)
                    dve.tensor_tensor(selfT[:], xhT[:], S[1][:], ALU.mult).then_inc(selfT_ready, 1)
                if t == L1["recv_elu"]:
                    elu(V_bank[1], cols[:, 1:2], exp1r, recvT, recv_exp, recv_min, recvT_ready, turn)
                if t == L1["residual"]:
                    dve.wait_ge(out1_psum, pair)
                    dve.tensor_tensor(X2[:], S[1][:].rearrange("p (r d) -> p r d", r=4), X1[:],
                                      ALU.add).then_inc(x2_ready, 1)

            def layer2(t, turn):
                pair = turn.at(1, 0)
                if t == LN2["stats"]:
                    dve.wait_ge(x2_ready, pair)
                stats(t, LN2, 1, X2, pair)
                if t == L2["mask"]:
                    dve.wait_ge(exp2_ready, pair)
                    dve.tensor_tensor(weight2[:], weight2[:], AT[:].unsqueeze(1).to_broadcast([P, 2, NB, N]),
                                      ALU.mult).then_inc(weight2_ready, 1)
                if t == L2["residual"]:
                    dve.wait_ge(agg2_psum, pair)
                    for y, bank_ in enumerate((S[0], V_bank[0])):
                        sums = bank_[:, 0:NB * (P + 1)].rearrange("p (r d) -> p r d", r=NB)
                        last = dve.reciprocal(inv2[:, NB * y:NB * y + NB], sums[:, :, P])
                    last.then_inc(inv2_ready, 1)
                    one_block()
                    dve.wait_ge(inv2_ready, pair)
                    for n in range(4):
                        bank_, r = (S[0], V_bank[0])[n // NB], n % NB
                        last = dve.scalar_tensor_tensor(X3[:, n], bank_[:, r * (P + 1):r * (P + 1) + P], inv2[:, n:n + 1],
                                                        X2[:, n], ALU.mult, ALU.add)
                    last.then_inc(x3_ready, 1)

            def layer3(t, turn):
                pair = turn.at(1, -1)
                if t == LN3["stats"]:
                    dve.wait_ge(x3_held, turn.at(16, -16))
                stats(t, LN3, 2, X3_held, pair)
                s, p = divmod(t - L3_AT, L3_PERIOD)
                if not 0 <= s < STEPS:
                    return
                for cols_, blocks_, _, gates, step, _ in layer3_parts(turn, s):
                    if p == L3["update"]:
                        dve.wait_ge(tr_ready, step)
                        dve.scalar_tensor_tensor(rh[:, cols_], tr[:, cols_], 1.0, h3T[:, cols_], ALU.add, ALU.mult).then_inc(rh_ready, 1)
                    if p == L3["state"]:
                        dve.wait_ge(cand_ready, step)
                        dve.tensor_tensor(diff[:, cols_], cand[:, cols_], h3T[:, cols_], ALU.subtract).then_inc(diff_ready, 1)
                        one_block()
                        dve.wait_ge(diff_ready, step)
                        dve.wait_ge(tz_ready, step)
                        dve.scalar_tensor_tensor(gated[:, cols_], tz[:, cols_], 1.0, diff[:, cols_], ALU.add,
                                                 ALU.mult).then_inc(gated_ready, 1)
                        one_block()
                        dve.wait_ge(gated_ready, step)
                        dve.scalar_tensor_tensor(h3T[:, cols_], gated[:, cols_], 0.5, h3T[:, cols_], ALU.mult,
                                                 ALU.add).then_inc(state_ready, 1)
                    if p == L3["back"] and s == STEPS - 1:
                        dve.wait_ge(state_psum, step)
                        dve.wait_ge(out_stored, turn.at(32, -48))
                        dve.tensor_tensor(OUT[:, blocks_], rows(gates[:, cols_]), X3_held[:, blocks_], ALU.add).then_inc(out_ready, 1)

            dve.memset(eps[:], LN_EPS)
            dve.memset(minus_one[:], -1.0)
            dve.memset(minus_half[:], -0.5).then_inc(dve_const, 1)
            pre(PRE["stats"], 0, 1)
            setup_layer0()
            pre(PRE["evacuate"], 0, 1)

            def body(turn):
                for t in range(LOTS):
                    y, p = divmod(t, LOTS_B)
                    if turn.has_main:
                        start_lot(turn, t)
                    if turn.m == 0:
                        setup_rest(t)
                    if turn.has_post[y]:
                        post(p, 1 - y, turn.at(2, y), turn.at(ROUNDS, y * ROUNDS // 2))
                    if turn.has_main and (y == 0 or turn.pre_next):
                        pre(p, 1 - y, turn.at(2, y + 2))
                    if turn.has_l12:
                        layer1(t, turn)
                        layer2(t, turn)
                    if turn.has_l3:
                        layer3(t, turn)
                    finish_lot()

            run_turns(dve, body)

        @block.scalar
        def _(act):
            def blocks(turn, t):
                y, p = divmod(t, LOTS_B)
                row, c = divmod(p, EC)
                place, rnd = t % RING, t // RING
                need(act, freed[place], turn.at(ROUNDS, rnd))
                if p == 0:
                    act.wait_ge(u_ready, turn.at(2, y + 1))
                for n in range(BLOCKS - ACT_BLOCKS[t], BLOCKS):
                    g, half = divmod(n, NB)
                    i = half * P + g * ROWS + row
                    last = act.activation(ring[:, place, g, half * N:(half + 1) * N], V_bank[y][:, c * N:(c + 1) * N], ACT.Relu,
                                          bias=U[:, y, c, i:i + 1])
                last.then_inc(by_act[place], 1)

            def pre(p, y, value):
                if p == PRE["norm"]:
                    act.wait_ge(pre_shift, value)
                    for r in range(NB):
                        last = act.activation(H0[:, y, r], X0[:, y, r], ACT.Relu, bias=shift0[:, r:r + 1], scale=rstd0[:, r:r + 1])
                    last.then_inc(h0_ready, 1)
                if p == PRE["copy"]:
                    act.wait_ge(h0T_psum, value)
                    act.activation(H0T[:, y], PA[:, 0:N], ACT.Copy).then_inc(h0T_ready, 1)
                if p == PRE["evacuate"]:
                    act.wait_ge(uv_psum, value)
                    for c in range(EC):
                        last = act.activation(U[:, y, c], PB[:, c * N:(c + 1) * N], ACT.Identity, bias=b0_col[:, c:c + 1])
                    last.then_inc(u_ready, 1)
                    act.activation(V[:, y], V_bank[y][:].rearrange("p (c n) -> p c n", c=EC), ACT.Copy).then_inc(v_ready, 1)

            def post(p, y, value):
                if p == POST["exp"]:
                    act.wait_ge(exp_bias_ready, value)
                    for r in range(NB):
                        last = act.activation(prob[:, r], S[y][:, r * N:(r + 1) * N], ACT.Exp, bias=exp_bias[:, r:r + 1],
                                              accum_out=row_sum[:, r:r + 1])
                    last.then_inc(prob_ready, 1)
                if p == POST["copy"]:
                    act.wait_ge(probT_psum, value)
                    act.activation(probT[:], PB[:].rearrange("p (r i) -> p r i", r=NB), ACT.Copy).then_inc(probT_ready, 1)
                if p == POST["tanh"]:
                    act.wait_ge(attn_psum, value)
                    act.wait_ge(half_inv_ready, value)
                    for r in range(NB):
                        last = act.activation(tanh0[:, r], PA[:, r * P:(r + 1) * P], ACT.Tanh, scale=half_inv[:, r:r + 1])
                    last.then_inc(tanh0_ready, 1)

            def norm(t, ln, n, src, dst, pair):
                if t == ln["norm"]:
                    act.wait_ge(ln_shift[n], pair)
                    for r in range(4):
                        last = act.activation(dst[:, r], src[:, r], ACT.Relu, bias=shift[:, n, r:r + 1], scale=rstd[:, n, r:r + 1])
                    last.then_inc(h_ready[n], 1)

            def layer1(t, turn):
                pair = turn.at(1, 0)
                norm(t, LN1, 0, X1, h1, pair)
                if t == LN1["copy"]:
                    act.wait_ge(hT_psum[0], pair)
                    act.activation(h1T[:], S[1][:], ACT.Copy).then_inc(hT_ready[0], 1)
                if t == L1["exp"]:
                    act.wait_ge(xh_psum, pair)
                    act.activation(exp1[:], V_bank[1][:], ACT.Exp, bias=cols[:, 0:1]).then_inc(xh_exp, 1)
                if t == L1["edge_copy"]:
                    act.wait_ge(edge_psum, pair)
                    act.activation(xh[:], V_bank[1][:].rearrange("p (r d) -> p r d", r=4), ACT.Copy).then_inc(xh_ready, 1)
                if t == L1["tanh"]:
                    act.wait_ge(src_ready, pair)
                    for y in range(2):
                        for r in range(NB):
                            n = NB * y + r
                            last = act.activation(edge[:, y, r], S[1][:, y * N:(y + 1) * N], ACT.Tanh,
                                                  bias=src_bias[:, n:n + 1], scale=0.5)
                    last.then_inc(edge_tanh, 1)
                if t == L1["agg_copy"]:
                    act.wait_ge(agg1_psum, pair)
                    act.activation(aggT[:], V_bank[1][:], ACT.Copy).then_inc(aggT_ready, 1)
                if t == L1["recv_exp"]:
                    act.wait_ge(recv_psum, pair)
                    act.activation(exp1r[:], V_bank[1][:], ACT.Exp, bias=cols[:, 1:2]).then_inc(recv_exp, 1)

            def layer2(t, turn):
                pair = turn.at(1, 0)
                norm(t, LN2, 1, X2, h2, pair)
                if t == LN2["copy"]:
                    act.wait_ge(hT_psum[1], pair)
                    act.activation(h2T[:], V_bank[0][:], ACT.Copy).then_inc(hT_ready[1], 1)
                if t == L2["copy"]:
                    act.wait_ge(y_psum, pair)
                    act.activation(YT[:], S[0][:], ACT.Copy).then_inc(yT_ready, 1)
                    act.activation(HV[:, :, 0:P], V_bank[0][:].rearrange("p (r d) -> p r d", r=4), ACT.Copy).then_inc(hv_ready, 1)
                if t == L2["tanh"]:
                    act.wait_ge(logit_psum, pair)
                    for y, bank_ in enumerate((S[0], V_bank[0])):
                        last = act.activation(logit2[:, y], bank_[:].rearrange("p (r n) -> p r n", r=NB), ACT.Tanh,
                                              scale=float(P) ** -0.5 / LOGIT_BOUND2)
                    last.then_inc(tanh2_ready, 1)
                if t == L2["exp"]:
                    act.wait_ge(tanh2_ready, pair)
                    act.activation(weight2[:], logit2[:], ACT.Exp, scale=LOGIT_BOUND2).then_inc(exp2_ready, 1)

            def layer3(t, turn):
                pair = turn.at(1, -1)
                norm(t, LN3, 2, X3_held, h3, pair)
                if t == LN3["copy"]:
                    act.wait_ge(hT_psum[2], pair)
                    act.activation(h3T[:], R0[:], ACT.Copy).then_inc(hT_ready[2], 1)
                s, p = divmod(t - L3_AT, L3_PERIOD)
                if not 0 <= s < STEPS:
                    return
                for cols_, blocks_, messages, gates, step, _ in layer3_parts(turn, s):
                    if p == L3["copy"]:
                        act.wait_ge(m_psum, step)
                        act.activation(mT[:, cols_], messages[:, cols_], ACT.Copy).then_inc(mT_ready, 1)
                    if p == L3["reset"]:
                        act.wait_ge(r_psum, step)
                        act.activation(tr[:, cols_], gates[:, cols_], ACT.Tanh, bias=bias3[:, 1:2], scale=0.5).then_inc(tr_ready, 1)
                    if p == L3["z_gate"]:
                        act.wait_ge(z_psum, step)
                        act.activation(tz[:, cols_], gates[:, cols_], ACT.Tanh, bias=bias3[:, 0:1], scale=0.5).then_inc(tz_ready, 1)
                    if p == L3["tanh"]:
                        act.wait_ge(cand_psum, step)
                        act.activation(cand[:, cols_], messages[:, cols_], ACT.Tanh, bias=bias3[:, 2:3]).then_inc(cand_ready, 1)
                    if p == L3["back"] and s < STEPS - 1:
                        act.wait_ge(state_psum, step)
                        act.activation(h3[:, blocks_], rows(gates[:, cols_]), ACT.Copy).then_inc(state_back, 1)

            for p in sorted(PRE.values()):
                pre(p, 0, 1)

            def body(turn):
                for t in range(LOTS):
                    y, p = divmod(t, LOTS_B)
                    if turn.has_main:
                        blocks(turn, t)
                    if turn.m == 0 and t == SETUP_REST["ready"]:
                        act.wait_ge(loaded_rest, 16 * LOADS_REST)
                        act.wait_ge(dve_rest_const, DVE_REST_ALL)
                    if turn.has_post[y]:
                        post(p, 1 - y, turn.at(2, y))
                    if turn.has_main and (y == 0 or turn.pre_next):
                        pre(p, 1 - y, turn.at(2, y + 2))
                    if turn.has_l12:
                        layer1(t, turn)
                        layer2(t, turn)
                    if turn.has_l3:
                        layer3(t, turn)

            run_turns(act, body)

        @block.tensor
        def _(pe):
            def mm(dst, lhsT, rhs, start=True, stop=True):
                return pe.matmul(dst, lhsT, rhs, start=start, stop=stop)

            def setup_layer0():
                pe.wait_ge(gp_const, 2)
                pe.wait_ge(loaded, 16 * LOADS0)
                for j in range(NB):
                    for i in range(NB):
                        last = pe.transpose(R0[:, j * N + i * P:j * N + (i + 1) * P], A[:, i, j * P:(j + 1) * P], ident[:])
                last.then_inc(pe_const, 1)
                pe.wait_ge(dve_const, DVE_CONST_A_LIN)
                for j in range(2):
                    for c in range(EC):
                        mm(R1[:, j:j + 1], A[:, c, j * P:(j + 1) * P], a_lin[:, c:c + 1], c == 0, c == EC - 1)
                for c in range(EC):
                    last = mm(R1[:, 2:3], a_lin_wide[:, c], b0_col[:, c:c + 1], c == 0, c == EC - 1)
                last.then_inc(pe_const, 1)

            def setup_rest(t):
                if t == SETUP_REST["transpose"]:
                    pe.wait_ge(loaded_rest, 16 * LOADS_REST)
                    for n, w in enumerate((raw2[:, 0], raw2[:, 1], rawu[:, 0], rawu[:, 1])):
                        pe.transpose(R1[:, n * P:(n + 1) * P], w, ident[:])
                    for n in range(3):
                        for half in range(2):
                            last = mm(R0[:, n * P:(n + 1) * P], raw3[:, n, half * P:(half + 1) * P], ident[:], half == 0, half == 1)
                    last.then_inc(pe_rest_const, 1)
                if t == SETUP_REST["product"]:
                    pe.wait_ge(dve_rest_const, DVE_REST_TURNED)
                    mm(R0[:, 0:P], qT, kT).then_inc(pe_rest_const, 1)
                if t == SETUP_REST["ready"]:
                    pe.wait_ge(dve_rest_const, DVE_REST_ALL)

            def lot(turn, t):
                y, p = divmod(t, LOTS_B)
                row, c = divmod(p, EC)
                place, rnd = t % RING, t // RING
                if p == 0:
                    need(pe, prob_ready, turn.at(2, y - 1))
                    if y == 0:
                        need(pe, x3_ready, turn.at(1, -1))
                    elif turn.has_l12:
                        pe.wait_ge(x2_ready, turn.at(1, 0))
                    pe.wait_ge(h0T_ready, turn.at(2, y + 1))
                    pe.matmul(S[y][:].rearrange("p (r j) -> p r j", r=NB), w2_lin_wide[:],
                              H0T[:, y].unsqueeze(1).to_broadcast([P, NB, N]), start=True, stop=False,
                              skip_group_check=True)
                    pe.matmul(S[y][:].rearrange("p (r j) -> p r j", r=NB), ident[:], A_bias[:], start=False, stop=False,
                              skip_group_check=True)
                pe.wait_ge(by_dve[place], turn.at(ROUNDS, rnd + 1))
                pe.wait_ge(by_act[place], turn.at(ROUNDS, rnd + 1))
                for g in range(GROUPS):
                    last = pe.matmul(S[y][g * ROWS:(g + 1) * ROWS, :], a_window[:, c, ROWS - 1 - row:2 * ROWS - 1 - row],
                                     ring[:, place, g], start=False, stop=p == LOTS_B - 1, skip_group_check=True)
                last.then_inc(freed[place], 1)

            def pre(p, y, value, bank_read=None):
                if p == PRE["transpose"]:
                    pe.wait_ge(h0_ready, value)
                    for r in range(NB):
                        last = pe.transpose(PA[:, r * P:(r + 1) * P], H0[:, y, r], ident[:])
                    last.then_inc(h0T_psum, 1)
                if p == PRE["project"]:
                    pe.wait_ge(h0T_ready, value)
                    if bank_read is not None:
                        pe.wait_ge(*bank_read)
                    for r in range(NB):
                        mm(PA[:, N + r:N + r + 1], H0T[:, y, r * P:(r + 1) * P], w_lin[:, 0:1])
                    for j, bank_ in enumerate((PB, V_bank[y])):
                        for c in range(EC):
                            last = mm(bank_[:, c * N:(c + 1) * N], AT[:, j, c * P:(c + 1) * P], H0T[:, y])
                    last.then_inc(uv_psum, 1)

            def post(p, y, value):
                if p == POST["transpose"]:
                    pe.wait_ge(prob_ready, value)
                    for j in range(NB):
                        for i in range(NB):
                            last = pe.transpose(PB[:, j * N + i * P:j * N + (i + 1) * P], prob[:, i, j * P:(j + 1) * P], ident[:])
                    last.then_inc(probT_psum, 1)
                if p == POST["aggregate"]:
                    pe.wait_ge(probT_ready, value)
                    for i in range(NB):
                        for j in range(NB):
                            last = mm(PA[:, i * P:(i + 1) * P], probT[:, j, i * P:(i + 1) * P], H0[:, y, j], j == 0, j == NB - 1)
                    last.then_inc(attn_psum, 1)

            def turn_blocks(n, bank_):
                for r in range(4):
                    last = pe.transpose(bank_[:, r * P:(r + 1) * P], (h1, h2, h3)[n][:, r], ident[:])
                last.then_inc(hT_psum[n], 1)

            def layer1(t, turn):
                pair = turn.at(1, 0)
                if t == LN1["transpose"]:
                    pe.wait_ge(h_ready[0], pair)
                    turn_blocks(0, S[1])
                if t == L1["project"]:
                    pe.wait_ge(hT_ready[0], pair)
                    mm(V_bank[1][:], Wi[:], h1T[:]).then_inc(xh_psum, 1)
                if t == L1["edge_terms"]:
                    pe.wait_ge(xhT_ready, pair)
                    mm(S[1][:], We_tgt_wide[:], xhT[:])
                    for n in range(4):
                        mm(PA[:, SRC_COLS.start + n:SRC_COLS.start + n + 1], xhT[:, n * P:(n + 1) * P], We[:, 0:1])
                    for n in range(4):
                        last = pe.transpose(V_bank[1][:, n * P:(n + 1) * P], xhT[:, n * P:(n + 1) * P], ident[:])
                    last.then_inc(edge_psum, 1)
                if t == L1["aggregate"]:
                    pe.wait_ge(xh_ready, pair)
                    pe.wait_ge(edge_ready, pair)
                    for y in range(2):
                        for r in range(NB):
                            mm(V_bank[1][:, y * N:(y + 1) * N], xh[:, NB * y + r], edge[:, y, r], r == 0, r == NB - 1)
                    for y in range(2):
                        for r in range(NB):
                            last = mm(S[1][:, y * N:(y + 1) * N], ones[:], edge[:, y, r], r == 0, r == NB - 1)
                    last.then_inc(agg1_psum, 1)
                if t == L1["receive"]:
                    pe.wait_ge(aggT_ready, pair)
                    mm(V_bank[1][:], Wn[:, 0], aggT[:], True, False)
                    pe.wait_ge(selfT_ready, pair)
                    mm(V_bank[1][:], Wn[:, 1], selfT[:], False, True).then_inc(recv_psum, 1)
                if t == L1["out"]:
                    pe.wait_ge(recvT_ready, pair)
                    for n in range(4):
                        mm(S[1][:, n * P:(n + 1) * P], ones[0:1, :], bm_half[:], True, False)
                        mm(S[1][:, n * P:(n + 1) * P], recvT[:, n * P:(n + 1) * P], Wm[:, 0], False, False)
                        last = mm(S[1][:, n * P:(n + 1) * P], xhT[:, n * P:(n + 1) * P], Wm[:, 1], False, True)
                    last.then_inc(out1_psum, 1)

            def layer2(t, turn):
                pair = turn.at(1, 0)
                if t == LN2["transpose"]:
                    pe.wait_ge(h_ready[1], pair)
                    turn_blocks(1, V_bank[0])
                if t == L2["project"]:
                    pe.wait_ge(hT_ready[1], pair)
                    pe.wait_ge(prob_ready, turn.at(2, 1 if turn.has_main else 0))
                    mm(S[0][:], G[:], h2T[:])
                    for n in range(4):
                        last = mm(V_bank[0][:, n * P:(n + 1) * P], h2T[:, n * P:(n + 1) * P], Wv[:])
                    last.then_inc(y_psum, 1)
                if t == L2["scores"]:
                    pe.wait_ge(yT_ready, pair)
                    pe.wait_ge(hv_ready, pair)
                    for y, bank_ in enumerate((S[0], V_bank[0])):
                        for r in range(NB):
                            n = NB * y + r
                            last = mm(bank_[:, r * N:(r + 1) * N], h2T[:, n * P:(n + 1) * P], YT[:, y * N:(y + 1) * N])
                    last.then_inc(logit_psum, 1)
                if t == L2["aggregate"]:
                    pe.wait_ge(weight2_ready, pair)
                    for y, bank_ in enumerate((S[0], V_bank[0])):
                        for i in range(NB):
                            for r in range(NB):
                                last = mm(bank_[:, i * (P + 1):(i + 1) * (P + 1)], weight2[:, y, r, i * P:(i + 1) * P],
                                          HV[:, NB * y + r], r == 0, r == NB - 1)
                    last.then_inc(agg2_psum, 1)

            def layer3(t, turn):
                pair = turn.at(1, -1)
                if t == LN3["transpose"]:
                    pe.wait_ge(h_ready[2], pair)
                    turn_blocks(2, R0)
                s, p = divmod(t - L3_AT, L3_PERIOD)
                if not 0 <= s < STEPS:
                    return
                for cols_, blocks_, messages, gates, step, back in layer3_parts(turn, s):
                    if p == L3["message"]:
                        if s == 0:
                            pe.wait_ge(hT_ready[2], pair)
                        else:
                            pe.wait_ge(state_back, back)
                        for n in range(blocks_.start, blocks_.stop, NB):
                            for r in range(NB):
                                last = mm(messages[:, n * P:(n + NB) * P], h3[:, n + r], AT[:, r], r == 0, r == NB - 1)
                        last.then_inc(m_psum, 1)
                    if p == L3["gates"]:
                        pe.wait_ge(mT_ready, step)
                        mm(gates[:, cols_], W345[:, 1], mT[:, cols_], True, False)
                        mm(gates[:, cols_], u3T, h3T[:, cols_], False, True).then_inc(r_psum, 1)
                        mm(messages[:, cols_], W345[:, 2], mT[:, cols_], True, False)
                    if p == L3["candidate"]:
                        pe.wait_ge(tr_ready, step)
                        pe.matmul(gates[:, cols_], W345[:, 0], mT[:, cols_], start=False, stop=True,
                                  skip_group_check=True).then_inc(z_psum, 1)
                        pe.wait_ge(rh_ready, step)
                        mm(messages[:, cols_], u5T_half, rh[:, cols_], False, True).then_inc(cand_psum, 1)
                    if p == L3["transpose"]:
                        pe.wait_ge(state_ready, step)
                        pe.wait_ge(tz_ready, step)
                        for n in range(blocks_.start, blocks_.stop):
                            last = pe.transpose(gates[:, n * P:(n + 1) * P], h3T[:, n * P:(n + 1) * P], ident[:])
                        last.then_inc(state_psum, 1)

            setup_layer0()
            pre(PRE["transpose"], 0, 1)
            pe.wait_ge(dve_const, DVE_CONST_ALL)
            pre(PRE["project"], 0, 1)

            def body(turn):
                for t in range(LOTS):
                    if turn.has_main:
                        lot(turn, t)
                    t += LEAD
                    if t >= LOTS:
                        continue
                    y, p = divmod(t, LOTS_B)
                    if turn.m == 0:
                        setup_rest(t)
                    if turn.has_post[y]:
                        post(p, 1 - y, turn.at(2, y))
                    if turn.has_main and (y == 0 or turn.pre_next):
                        pre(p, 1 - y, turn.at(2, y + 2), (x3_ready if y else recvT_ready, turn.at(1, 0)) if turn.has_l12 else None)
                    if turn.has_l12:
                        layer1(t, turn)
                        layer2(t, turn)
                    if turn.has_l3:
                        layer3(t, turn)

            run_turns(pe, body)


_INS = ["x", "adj", "L0_gnn_b_lin", "L0_gnn_a", "L1_gnn_Wi", "L1_gnn_bi", "L1_gnn_We", "L1_gnn_be", "L1_gnn_Wn",
        "L1_gnn_bn", "L1_gnn_Wm", "L1_gnn_bm", "L2_gnn_q", "L2_gnn_k", "L2_gnn_v", "L3_gnn_w3_w", "L3_gnn_w3_b",
        "L3_gnn_u3_w", "L3_gnn_u3_b", "L3_gnn_w4_w", "L3_gnn_w4_b", "L3_gnn_w5_w", "L3_gnn_w5_b", "L3_gnn_u5_w",
        "L3_gnn_u5_b"]


def kernel(**inputs):
    import numpy as np
    import concourse.bacc as bacc
    from concourse.bass_utils import run_bass_kernel_spmd

    nc = bacc.Bacc("TRN2", target_bir_lowering=False, num_devices=1)
    arrays, args = {}, []
    for name in _INS:
        a = np.ascontiguousarray(inputs[name])
        arrays[f"in_{name}"] = a
        args.append(nc.dram_tensor(f"in_{name}", a.shape, mybir.dt.from_np(a.dtype), kind="ExternalInput").ap())
    out = nc.dram_tensor("out", inputs["x"].shape, F32, kind="ExternalOutput").ap()
    gnn_stack(nc, *args, out)
    results = run_bass_kernel_spmd(nc, [arrays], core_ids=[0])
    return results.results[0]["out"]
```
